# Optimizing a Trainium2 kernel written in Bass

```python
import numpy as np
import jax
import jax.numpy as jnp

def _softmax(x, axis=-1):
    return jax.nn.softmax(x, axis=axis)

def _gelu(x):
    return jax.nn.gelu(x, approximate=True)

def _silu(x):
    return jax.nn.silu(x)

def _sigmoid(x):
    return jax.nn.sigmoid(x)

def _layernorm(x, axis=-1, eps=1e-05):
    m = jnp.mean(x, axis=axis, keepdims=True)
    v = jnp.var(x, axis=axis, keepdims=True)
    return (x - m) / jnp.sqrt(v + eps)

def _scatter_add(tgt, idx, src, axis=0):
    return tgt.at[idx].add(src)

def _segment_sum(src, seg, n):
    return jax.ops.segment_sum(src, seg, n)
kernel_name = 'mk_gnn_preln_d1_gnn_r32_7f1e64'

def setup_inputs(seed: int=0):
    np.random.seed(seed)
    _w = jnp.asarray

    def _rec_inputs():
        import jax
        import jax.numpy as jnp
        _gk = jax.random.key(seed)
        x = -0.0003929 + 0.9999 * jax.random.normal(jax.random.fold_in(_gk, 1), (512, 1024), jnp.float32)
        _s = jax.random.randint(jax.random.fold_in(_gk, 2), (4096,), 0, 512, jnp.int32)
        _d = jax.random.randint(jax.random.fold_in(_gk, 3), (4096,), 0, 512, jnp.int32)
        _loop = jnp.arange(512, dtype=jnp.int32)
        src = jnp.concatenate([_s, _d, _loop])
        dst = jnp.concatenate([_d, _s, _loop])
        _o = jnp.argsort(dst, stable=True)
        src = src[_o]
        dst = dst[_o]
        return (x, src, dst)
    x, src, dst = _rec_inputs()

    def _L0_gnn_setup():
        import jax, jax.numpy as jnp
        import numpy as np
        NH, NO = (128, 384)
        N = NH + NO
        E_HH, E_OO, E_HO = (256, 1280, 512)
        E = E_HH + E_OO + E_HO
        D = 1024
        key = jax.random.key(seed)
        ks = jax.random.split(key, 12)
        w = lambda k, s: jax.random.normal(k, s, jnp.float32) * 0.02
        return {'n_f': jax.random.normal(ks[0], (N, D), jnp.float32), 'W_hh': w(ks[1], (2 * D, D)), 'b_hh': jnp.zeros((D,), jnp.float32), 'W_oo': w(ks[2], (2 * D, D)), 'b_oo': jnp.zeros((D,), jnp.float32), 'W_ho': w(ks[3], (2 * D, D)), 'b_ho': jnp.zeros((D,), jnp.float32), 'W_a': w(ks[4], (D, 1)), 'b_a': jnp.zeros((1,), jnp.float32), 'W_hn': w(ks[5], (2 * D, D)), 'b_hn': jnp.zeros((D,), jnp.float32), 'W_on': w(ks[6], (2 * D, D)), 'b_on': jnp.zeros((D,), jnp.float32), 'edge_src': jax.random.randint(ks[7], (E,), 0, N, jnp.int32), 'edge_dst': jax.random.randint(ks[8], (E,), 0, N, jnp.int32)}
    _L0_gnn_all = _L0_gnn_setup()
    _L0_gnn_in = {k: v for k, v in _L0_gnn_all.items() if k in ('W_hh', 'b_hh', 'W_oo', 'b_oo', 'W_ho', 'b_ho', 'W_a', 'b_a', 'W_hn', 'b_hn', 'W_on', 'b_on')}
    del _L0_gnn_all
    return {'x': x, 'src': src, 'dst': dst, 'L0_gnn_W_hh': _L0_gnn_in['W_hh'], 'L0_gnn_b_hh': _L0_gnn_in['b_hh'], 'L0_gnn_W_oo': _L0_gnn_in['W_oo'], 'L0_gnn_b_oo': _L0_gnn_in['b_oo'], 'L0_gnn_W_ho': _L0_gnn_in['W_ho'], 'L0_gnn_b_ho': _L0_gnn_in['b_ho'], 'L0_gnn_W_a': _L0_gnn_in['W_a'], 'L0_gnn_b_a': _L0_gnn_in['b_a'], 'L0_gnn_W_hn': _L0_gnn_in['W_hn'], 'L0_gnn_b_hn': _L0_gnn_in['b_hn'], 'L0_gnn_W_on': _L0_gnn_in['W_on'], 'L0_gnn_b_on': _L0_gnn_in['b_on']}

def reference(x, src, dst, L0_gnn_W_hh, L0_gnn_b_hh, L0_gnn_W_oo, L0_gnn_b_oo, L0_gnn_W_ho, L0_gnn_b_ho, L0_gnn_W_a, L0_gnn_b_a, L0_gnn_W_hn, L0_gnn_b_hn, L0_gnn_W_on, L0_gnn_b_on):
    import jax
    import jax.numpy as jnp

    def _L0_gnn_ref(n_f, W_hh, b_hh, W_oo, b_oo, W_ho, b_ho, W_a, b_a, W_hn, b_hn, W_on, b_on, edge_src, edge_dst):
        import jax, jax.numpy as jnp
        import numpy as np
        NH, NO = (128, 384)
        N = NH + NO
        E_HH, E_OO, E_HO = (256, 1280, 512)
        E = E_HH + E_OO + E_HO
        D = 1024
        feat = jnp.concatenate([n_f[edge_src], n_f[edge_dst]], axis=1)
        e_hh = jax.nn.relu(feat[:E_HH] @ W_hh + b_hh)
        e_oo = jax.nn.relu(feat[E_HH:E_HH + E_OO] @ W_oo + b_oo)
        e_ho = jax.nn.relu(feat[E_HH + E_OO:] @ W_ho + b_ho)
        e_f = jnp.concatenate([e_hh, e_oo, e_ho], axis=0)
        logit = (e_f @ W_a + b_a)[:, 0]
        m = jax.lax.stop_gradient(jax.ops.segment_max(logit, edge_dst, num_segments=N))
        ex = jnp.exp(logit - m[edge_dst])
        den = jax.ops.segment_sum(ex, edge_dst, num_segments=N)
        alpha = ex / den[edge_dst]
        z_f = jax.ops.segment_sum(alpha[:, None] * n_f[edge_src], edge_dst, num_segments=N)
        nf2 = jnp.concatenate([n_f, z_f], axis=1)
        h_new = jax.nn.relu(nf2[:NH] @ W_hn + b_hn)
        o_new = jax.nn.relu(nf2[NH:] @ W_on + b_on)
        return jnp.concatenate([h_new, o_new], axis=0)
    h = jnp.maximum(_layernorm(x, axis=-1), 0.0)
    x = x + _L0_gnn_ref(h, L0_gnn_W_hh, L0_gnn_b_hh, L0_gnn_W_oo, L0_gnn_b_oo, L0_gnn_W_ho, L0_gnn_b_ho, L0_gnn_W_a, L0_gnn_b_a, L0_gnn_W_hn, L0_gnn_b_hn, L0_gnn_W_on, L0_gnn_b_on, src, dst)
    return x

_drawn_inputs = setup_inputs


def setup_inputs(seed=0):
    import zlib

    import numpy as np

    out = dict(_drawn_inputs(seed))
    spreads = {'L0_gnn_b_hh': (0.0, 2.0),
     'L0_gnn_b_oo': (0.0, 2.0),
     'L0_gnn_b_ho': (0.0, 0.8),
     'L0_gnn_b_hn': (0.0, 0.1),
     'L0_gnn_b_on': (0.0, 0.1)}
    factors = {'L0_gnn_W_hh': 8.0, 'L0_gnn_W_oo': 8.0, 'L0_gnn_W_ho': 6.667, 'L0_gnn_W_a': 6.285}
    for name, (base, spread) in spreads.items():
        noise = np.random.default_rng([zlib.crc32(name.encode()), seed]).standard_normal(out[name].shape)
        drawn = base * np.exp(spread * noise) if base else spread * noise
        out[name] = jnp.asarray(drawn.astype(out[name].dtype))
    for name, factor in factors.items():
        out[name] = (out[name] * factor).astype(out[name].dtype)
    return out
```

```python
import concourse.bass as bass
from concourse import mybir
from contextlib import ExitStack

P = 128
N, D = 512, 1024
NB = N // P
KT = D // P
HALF = 512
NHALF = D // HALF
E_HH, E_OO = 256, 1280
E_HO = 8704 - E_HH - E_OO
T_HH, T_OO, T_HO = E_HH // P, E_OO // P, E_HO // P
T_ALL = T_HO + T_OO + T_HH
T_NODE = T_HO + T_OO
KC = 4
PH_HO, PH_OO, PH_HH, PH_TOP, PH_BOT = 0, 8, 16, 24, 32
CHUNKS = 40
RAW = 4
SPLIT = 2
SLOTS = 4
EMPTY = -3.0e38
TINY = 1.0e-30
EPS = 1e-5


def build(nc, x, src, dst, w_chunks, biases, w_a, b_a, out):
    f32, f32r, bf16, f16 = mybir.dt.float32, mybir.dt.float32r, mybir.dt.bfloat16, mybir.dt.float16
    i32, i16 = mybir.dt.int32, mybir.dt.int16
    ALU = mybir.AluOpType
    ACT = mybir.ActivationFunctionType
    AX = mybir.AxisListType

    def dram(name, shape):
        return nc.dram_tensor(name, shape, f32, kind="Internal").ap()

    h_dram = dram("h_dram", (N, D))
    node_tab = {"ho": (dram("p_ho", (N, D)), dram("q_ho", (N, D))),
                "oo": (dram("p_oo", (N, D)), dram("q_oo", (N, D)))}
    pair_tab = {k: dram(f"pairs_{k}", (N * N, 1)) for k in ("ho", "oo", "hh")}

    with ExitStack() as ctx:
        def sb(name, shape, dt):
            return ctx.enter_context(nc.sbuf_tensor(name, shape, dt))

        def shared(*specs):
            got = []
            for spec in specs[:-1]:
                with nc.sbuf_tensor(*spec) as t:
                    got.append(t)
            return got + [sb(*specs[-1])]

        def sem(name):
            return ctx.enter_context(nc.semaphore(name))

        h_t = sb("h_t", [P, 2, KT, N], f32r)
        h_n = h_t[:, :, :, :].rearrange("p s (b c) n -> p s b (c n)", b=NB)
        raw = sb("raw", [P, RAW, KC, HALF], f32)
        w_hi = sb("w_hi", [P, SPLIT, KC, HALF], f32r)
        w_lo = sb("w_lo", [P, SPLIT, KC, HALF], f32r)
        z_t, gath = shared(("z_t", [P, 2, KT, N], f32r), ("gath", [P, 2, SLOTS, D], f32))
        feat_hi, partial = shared(("feat_hi", [P, 2 * KT, E_HH], f32r), ("partial", [P, NB, D], f32))
        feat_lo, att_t, h_sb = shared(("feat_lo", [P, 2 * KT, E_HH], f32r), ("att_t", [P, 2, NB, N], f32r),
                                      ("h_sb", [P, NB, D], f32))
        onehot, stage = shared(("onehot", [P, 2, 2, 2, N], bf16), ("stage", [P, 2, NB, HALF], f32))
        counts = sb("counts", [P, 3, NB, N], i16)
        bias = sb("bias", [P, 2, D], f32)
        wa = sb("wa", [P, D], f32)
        ba = sb("ba", [P, 1], f32)
        ident = sb("ident", [P, P], f32)
        zeros = sb("zeros", [P, P], f16)
        node_row = sb("node_row", [P, N], f16)
        i_src = sb("i_src", [P, T_ALL], i32)
        i_dst = sb("i_dst", [P, T_ALL], i32)
        f_src = sb("f_src", [P, T_ALL], f32)
        f_dst = sb("f_dst", [P, T_ALL], f32)
        index = sb("index", [P, T_NODE + SLOTS, 3], i32)
        pair_hh = sb("pair_hh", [P, T_HH], i32)
        index_now = sb("index_now", [P, SLOTS, 3], i32)
        logit = sb("logit", [P, SLOTS], f32)
        logit_out = sb("logit_out", [P, SLOTS], f32)
        logit_half = sb("logit_half", [P, NHALF, T_HH], f32)
        logit_hh = sb("logit_hh", [P, T_HH], f32)
        logit_hh_out = sb("logit_hh_out", [P, T_HH], f32)
        stats = sb("stats", [P, NB, 2, 6], f32)
        mv = sb("mv", [P, NB, 2], f32)
        rstd = sb("rstd", [P, 4, NB], f32)
        peak = sb("peak", [P, 4, NB], f32)
        den = sb("den", [P, 2, NB], f32)

        edge_p, edge_q = gath[:, 0], gath[:, 1]
        x_sb = gath[:, 0]
        hh_rows = gath[:, 1]
        tab_sb = [gath[:, 0, 0:2, :].rearrange("p a (b n) -> p (a b) n", n=N),
                  gath[:, 0, 2:4, :].rearrange("p a (b n) -> p (a b) n", n=N),
                  gath[:, 1, 0:2, :].rearrange("p a (b n) -> p (a b) n", n=N)]
        att = gath[:, 1, 2:4, :].rearrange("p a (b n) -> p (a b) n", n=N)
        bank = [ctx.enter_context(nc.psum_tensor(f"bank{i}", [P, HALF], f32)) for i in range(8)]

        s_x, s_idx, s_const, s_bias, s_tabs = sem("x_landed"), sem("indices_landed"), sem("constants_landed"), sem("bias_landed"), sem("pair_tables_cleared")
        s_empty, s_iota, s_index = sem("empty_ready"), sem("iota_ready"), sem("index_ready")
        s_var, s_std, s_norm, s_h = sem("variance_ready"), sem("std_ready"), sem("norm_ready"), sem("h_ready")
        s_hd, s_hh_rows = sem("h_stored"), sem("hh_rows_landed")
        s_tr, s_thi, s_tlo = sem("transposed"), sem("transposed_hi"), sem("transposed_lo")
        s_raw = [sem(f"raw_landed{i}") for i in range(RAW)]
        s_whi, s_wlo, s_wused = sem("weights_hi"), sem("weights_lo"), sem("weights_used")
        s_pev, s_qev = sem("p_evacuated"), sem("q_evacuated")
        s_pst, s_qst = sem("p_stored"), sem("q_stored")
        s_one, s_oused, s_cnt, s_cev = sem("onehot_ready"), sem("onehot_used"), sem("counted"), sem("counts_evacuated")
        s_gath = [sem(f"edge_rows_landed{i}") for i in range(SLOTS)]
        s_now, s_esum, s_logit, s_scat = sem("index_now_ready"), sem("edge_summed"), sem("logit_ready"), sem("logits_scattered")
        s_hhlog, s_hhout, s_hhscat = sem("hh_logits_ready"), sem("hh_logits_out"), sem("hh_scattered")
        s_hhev, s_hhhalf = sem("hh_evacuated"), sem("hh_half_logits")
        s_part = sem("partial_ready")
        s_hre, s_xre = sem("h_reloaded"), sem("x_reloaded")
        s_tab = [sem(f"table_loaded_{kind}") for kind in pair_tab]
        s_hnhi, s_hn = sem("h_hi_ready"), sem("h_split")
        s_peak, s_exp, s_att, s_attr = sem("peak_ready"), sem("exp_ready"), sem("att_ready"), sem("att_transposed")
        s_athi, s_atlo, s_z, s_zhi, s_zlo = sem("att_hi"), sem("att_lo"), sem("z_ready"), sem("z_hi"), sem("z_lo")
        s_out, s_stored = sem("out_ready"), sem("out_stored")
        s_dve, s_turn = sem("vector_step"), sem("pool_turns")

        block = ctx.enter_context(nc.Block())

        def blocks(t):
            return t.rearrange("(b p) d -> p b d", p=P)

        @block.sync
        def _(sp):
            sp.dma_start(x_sb, blocks(x)).then_inc(s_x, 16)
            for c in range(RAW):
                sp.dma_start(raw[:, c], w_chunks[c]).then_inc(s_raw[c], 16)
            sp.wait_ge(s_h, NB)
            sp.dma_start(blocks(h_dram), h_sb[:, :, :]).then_inc(s_hd, 16)
            with sp.Fori(1, CHUNKS // RAW) as i:
                for s in range(RAW):
                    sp.wait_ge(s_wlo, RAW * i + (s + 1 - RAW))
                    sp.dma_start(raw[:, s], w_chunks[bass.ds(RAW * i + s, 1)].rearrange("o p k n -> (o p) k n")
                                 ).then_inc(s_raw[s], 16)
            for half in range(NHALF):
                for b in range(NB):
                    sp.wait_ge(s_out, NB * half + b + 1)
                    sp.dma_start(out[b * P:(b + 1) * P, half * HALF:(half + 1) * HALF],
                                   partial[:, b, half * HALF:(half + 1) * HALF]).then_inc(s_stored, 16)
            sp.wait_ge(s_stored, 16 * NHALF * NB)

        @block.scalar
        def _(act):
            for t0, tiles, e0 in ((0, T_HO, E_HH + E_OO), (T_HO, T_OO, E_HH), (T_NODE, T_HH, 0)):
                for to, of in ((i_src, src), (i_dst, dst)):
                    act.dma_start(to[:, t0:t0 + tiles], of[e0:e0 + tiles * P].rearrange("(p t) -> p t", p=P)
                                  ).then_inc(s_idx, 16)
            act.dma_start(wa[:, :], w_a.to_broadcast((P, D))).then_inc(s_const, 16)
            act.dma_start(ba[:, :], b_a.to_broadcast((P, 1))).then_inc(s_const, 16)
            for n in range(2):
                act.dma_start(bias[:, n], biases[n:n + 1, :].to_broadcast((P, D))).then_inc(s_bias, 16)

            act.wait_ge(s_var, 1)
            nc.scalar.activation(rstd[:, 1], rstd[:, 0], ACT.Sqrt).then_inc(s_std, 1)
            act.wait_ge(s_norm, 1)
            for b in range(NB):
                nc.scalar.activation(h_sb[:, b], x_sb[:, b], ACT.Relu, bias=rstd[:, 3, b:b + 1],
                                     scale=rstd[:, 2, b:b + 1]).then_inc(s_h, 1)
            act.wait_ge(s_empty, 1)
            for t in pair_tab.values():
                act.dma_start(t.rearrange("(p n) o -> p (n o)", p=P), stage[:, 0].rearrange("p b n -> p (b n)")
                              ).then_inc(s_tabs, 16)
            for k in range(KT):
                act.wait_ge(s_tr, k + 1)
                nc.scalar.activation(h_t[:, 0, k], bank[k][:, :], ACT.Copy).then_inc(s_thi, 1)
            act.sem_inc(s_qev, 1)

            def split_hi(c):
                act.wait_ge(s_raw[c % RAW], 16 * (c // RAW + 1))
                if c >= SPLIT:
                    act.wait_ge(s_wused, c - SPLIT + 1)
                nc.scalar.activation(w_hi[:, c % SPLIT], raw[:, c % RAW], ACT.Copy).then_inc(s_whi, 1)

            def store_half(tab, half, side):
                act.dma_start(blocks(tab)[:, :, half * HALF:(half + 1) * HALF], stage[:, side]
                              ).then_inc((s_pst, s_qst)[side], 16)

            def store_p(n, kind):
                act.wait_ge(s_pev, n + 2)
                store_half(node_tab[kind][0], n % 2, 0)

            def evacuate_q(n, kind):
                act.wait_ge(s_wused, 4 * (n + 1))
                if n:
                    act.wait_ge(s_qst, 16 * n)
                else:
                    act.wait_ge(s_tabs, 48)
                for b in range(NB):
                    i = nc.scalar.activation(stage[:, 1, b], bank[4 + b][:, :], ACT.Copy)
                i.then_inc(s_qev, 1)
                act.wait_ge(s_qev, n + 2)
                store_half(node_tab[kind][1], n % 2, 1)

            for c in range(4):
                split_hi(c)
            store_p(0, "ho")
            split_hi(4)
            split_hi(5)
            evacuate_q(0, "ho")
            split_hi(6)
            split_hi(7)
            store_p(1, "ho")
            act.dma_start(bias[:, 0], biases[2:3, :].to_broadcast((P, D))).then_inc(s_bias, 16)
            split_hi(8)
            evacuate_q(1, "ho")
            for k in range(KT):
                act.wait_ge(s_tr, KT + k + 1)
                nc.scalar.activation(feat_hi[:, 2 * k:2 * k + 2].rearrange("p k e -> p (k e)"), bank[k][:, :], ACT.Copy
                                     ).then_inc(s_thi, 1)
            split_hi(9)
            for kind, banks in ((0, 0), (1, 4), (2, 0)):
                act.wait_ge(s_cnt, kind + 1)
                for b in range(NB):
                    i = nc.scalar.activation(counts[:, kind, b], bank[banks + b][:, :], ACT.Copy)
                i.then_inc(s_cev, 1)
            for n in (2, 3):
                split_hi(4 * n + 2)
                split_hi(4 * n + 3)
                store_p(n, "oo")
                split_hi(4 * n + 4)
                evacuate_q(n, "oo")
                split_hi(4 * n + 5)
            for c in range(18, 26):
                split_hi(c)
            act.wait_ge(s_hhlog, 1)
            for n in range(2):
                act.dma_start(bias[:, n], biases[3 + n:4 + n, :].to_broadcast((P, D))).then_inc(s_bias, 16)
            act.dma_start(stage[:, 0], blocks(x)[:, :, 0:HALF]).then_inc(s_xre, 16)
            act.dma_start(stage[:, 1], blocks(x)[:, :, HALF:D]).then_inc(s_xre, 16)
            act.wait_ge(s_wused, PH_TOP)
            act.dma_start(h_sb[:, :, :], blocks(h_dram)).then_inc(s_hre, 16)
            for c in range(26, 34):
                split_hi(c)
            act.wait_ge(s_hre, 16)
            act.wait_ge(s_wused, PH_BOT)
            nc.scalar.activation(h_n[:, 0], h_sb[:, :, :], ACT.Copy).then_inc(s_hnhi, 1)

            act.wait_ge(s_peak, 1)
            for kind in range(3):
                for b in range(NB):
                    i = nc.scalar.activation(tab_sb[kind][:, b], tab_sb[kind][:, b], ACT.Exp,
                                             bias=peak[:, 3, b:b + 1])
                i.then_inc(s_exp, 1)
            for b in range(NB):
                act.wait_ge(s_attr, b + 1)
                if b == 0:
                    act.wait_ge(s_hn, 1)
                nc.scalar.activation(att_t[:, 0, b], bank[b][:, :], ACT.Copy).then_inc(s_athi, 1)
            for k in range(KT):
                act.wait_ge(s_z, k + 1)
                nc.scalar.activation(z_t[:, 0, k], bank[(k + 4) % 8][:, :], ACT.Copy).then_inc(s_zhi, 1)
            for c in range(34, CHUNKS):
                split_hi(c)

        @block.vector
        def _(dve):
            steps = [0]

            def step(i):
                steps[0] += 1
                i.then_inc(s_dve, 1)
                dve.wait_ge(s_dve, steps[0])

            dve.wait_ge(s_x, 16)
            for b in range(NB):
                for j in range(2):
                    i = nc.vector.bn_stats(stats[:, b, j], x_sb[:, b, j * HALF:(j + 1) * HALF])
            step(i)
            for b in range(NB):
                i = nc.vector.bn_aggr(mv[:, b], stats[:, b])
            step(i)
            nc.vector.tensor_scalar(rstd[:, 0], mv[:, :, 1], EPS, None, ALU.add).then_inc(s_var, 1)
            dve.wait_ge(s_std, 1)
            step(nc.vector.reciprocal(rstd[:, 2], rstd[:, 1]))
            step(nc.vector.tensor_tensor(rstd[:, 1], rstd[:, 2], rstd[:, 2], ALU.mult))
            step(nc.vector.tensor_tensor(rstd[:, 1], rstd[:, 1], rstd[:, 0], ALU.mult))
            step(nc.vector.tensor_scalar(rstd[:, 1], rstd[:, 1], -0.5, 1.5, ALU.mult, ALU.add))
            step(nc.vector.tensor_tensor(rstd[:, 2], rstd[:, 2], rstd[:, 1], ALU.mult))
            nc.vector.scalar_tensor_tensor(out=rstd[:, 3], in0=mv[:, :, 0], scalar=-1.0, in1=rstd[:, 2],
                                           op0=ALU.mult, op1=ALU.mult).then_inc(s_norm, 1)
            dve.wait_ge(s_idx, 16 * 6)
            step(nc.vector.memset(index[:, :, :], 0))
            nc.vector.tensor_copy(f_src[:, :], i_src[:, :])
            nc.vector.tensor_copy(f_dst[:, :], i_dst[:, :])
            step(nc.vector.tensor_copy(index[:, 0:T_NODE, 0], i_src[:, 0:T_NODE]))
            nc.vector.tensor_copy(index[:, 0:T_NODE, 1], i_dst[:, 0:T_NODE])
            nc.vector.scalar_tensor_tensor(out=index[:, SLOTS:SLOTS + T_NODE, 2], in0=f_dst[:, 0:T_NODE],
                                           scalar=float(N), in1=f_src[:, 0:T_NODE], op0=ALU.mult, op1=ALU.add)
            nc.vector.scalar_tensor_tensor(out=pair_hh[:, :], in0=f_dst[:, T_NODE:T_ALL], scalar=float(N),
                                           in1=f_src[:, T_NODE:T_ALL], op0=ALU.mult, op1=ALU.add).then_inc(s_index, 1)
            for k in range(KT):
                dve.wait_ge(s_thi, k + 1)
                nc.vector.tensor_tensor(h_t[:, 1, k], bank[k][:, :], h_t[:, 0, k].bitcast(f32), ALU.subtract
                                        ).then_inc(s_tlo, 1)

            def split_lo(c, slot=None):
                slot = c if slot is None else slot
                dve.wait_ge(s_whi, c + 1)
                nc.vector.tensor_tensor(w_lo[:, slot % SPLIT], raw[:, slot % RAW],
                                        w_hi[:, slot % SPLIT].bitcast(f32), ALU.subtract).then_inc(s_wlo, 1)

            def evacuate_p(n, half, slot):
                dve.wait_ge(s_wused, 4 * n + 2)
                for b in range(NB):
                    i = nc.vector.tensor_tensor(stage[:, 0, b], bank[b][:, :], bias[:, slot, bass.ds(half * HALF, HALF)],
                                                ALU.add)
                i.then_inc(s_pev, 1)

            def edge_logit(p, q, s, summed):
                dve.wait_ge(s_esum, summed)
                nc.vector.scalar_tensor_tensor(out=q, in0=p, scalar=0.0, in1=wa[:, :], op0=ALU.max, op1=ALU.mult,
                                               accum_out=logit[:, s:s + 1]).then_inc(s_logit, 1)

            def edges(n, t, s, landed):
                for j in range(n):
                    slot = (s + j) % SLOTS
                    dve.wait_ge(s_gath[slot], landed + 32 * ((s + j) // SLOTS))
                    p, q = edge_p[:, slot], edge_q[:, slot]
                    nc.vector.tensor_tensor(p, p, q, ALU.add).then_inc(s_esum, 1)
                    edge_logit(p, q, slot, t + j + 1)

            dve.sem_inc(s_pev, 1)
            for c in range(4):
                split_lo(c)
            dve.wait_ge(s_bias, 32)
            dve.wait_ge(s_tabs, 48)
            evacuate_p(0, 0, 0)
            for c in range(4, 8):
                split_lo(c)
            dve.wait_ge(s_pst, 16)
            evacuate_p(1, 1, 0)
            split_lo(8)
            for k in range(KT):
                dve.wait_ge(s_thi, KT + k + 1)
                nc.vector.tensor_tensor(feat_lo[:, 2 * k:2 * k + 2].rearrange("p k e -> p (k e)"), bank[k][:, :],
                                        feat_hi[:, 2 * k:2 * k + 2].rearrange("p k e -> p (k e)").bitcast(f32),
                                        ALU.subtract).then_inc(s_tlo, 1)
            split_lo(9)
            dve.wait_ge(s_const, 32)
            dve.wait_ge(s_iota, 1)
            dve.wait_ge(s_pst, 32)
            dve.wait_ge(s_qst, 32)

            def one_hot(g, slot, used):
                if used is not None:
                    dve.wait_ge(s_oused, used)
                for j in range(2):
                    for side, nodes in ((0, f_src), (1, f_dst)):
                        i = nc.vector.tensor_scalar(onehot[:, slot, j, side], node_row[:, :],
                                                    nodes[:, bass.ds(2 * g + j, 1)], None, ALU.is_equal)
                i.then_inc(s_one, 1)

            one_hot(0, 0, None)
            one_hot(1, 1, None)
            with dve.Fori(0, 4) as i:
                for s in range(SLOTS):
                    for j in range(2):
                        one_hot(8 * i + 2 * s + j + 2, j, 8 * i + 2 * s + j + 1)
                    edges(1, 4 * i + s, s, 32 * i + 32)
            with dve.Fori(0, 2) as i:
                for j in range(4):
                    edges(3, 16 + 12 * i + 3 * j, (3 * j) % SLOTS, 32 * (4 + 3 * i + 3 * j // SLOTS) + 32)
                    split_lo(10 + 4 * i + j, 10 + j)
                    if j == 1:
                        dve.wait_ge(s_pst, 32 + 16 * i)
                        dve.wait_ge(s_oused, 34)
                        evacuate_p(2 + i, i, 1)
            for half in range(NHALF):
                for j in range(4):
                    c = 18 + 4 * half + j
                    t = 40 + 8 * half + 2 * j
                    edges(2, t, t % SLOTS, 32 * (t // SLOTS) + 32)
                    split_lo(c)
                    if j == 3:
                        dve.wait_ge(s_bias, 48)
                        dve.wait_ge(s_pst, 64)
                        dve.wait_ge(s_qst, 64)
                        dve.wait_ge(s_wused, PH_HH + 4 * half + 4)
                        for e in range(T_HH):
                            i = nc.vector.tensor_tensor(stage[:, 0, e], bank[4 * half + e][:, :],
                                                        bias[:, 0, half * HALF:(half + 1) * HALF], ALU.add)
                        i.then_inc(s_hhev, 1)
                        dve.wait_ge(s_hhev, half + 1)
                        for e in range(T_HH):
                            i = nc.vector.scalar_tensor_tensor(out=stage[:, 1, e], in0=stage[:, 0, e], scalar=0.0,
                                                               in1=wa[:, half * HALF:(half + 1) * HALF],
                                                               op0=ALU.max, op1=ALU.mult,
                                                               accum_out=logit_half[:, half, e:e + 1])
                        i.then_inc(s_hhhalf, 1)
                        dve.wait_ge(s_hhhalf, half + 1)
            nc.vector.tensor_tensor(logit_hh[:, :], logit_half[:, 0], logit_half[:, 1], ALU.add).then_inc(s_hhlog, 1)
            dve.wait_ge(s_bias, 80)
            t = T_HO
            for j in range(8):
                n = 2 if j < 2 else 1
                edges(n, t, t % SLOTS, 32 * (t // SLOTS) + 32)
                t += n
                split_lo(26 + j)
                if j in (3, 7):
                    half = j // 4
                    dve.wait_ge(s_wused, PH_TOP + 4 * half + 4)
                    for b in range(NB):
                        i = nc.vector.tensor_tensor(partial[:, b, half * HALF:(half + 1) * HALF], bank[4 * half + b][:, :],
                                                    bias[:, min(b, 1), half * HALF:(half + 1) * HALF], ALU.add)
                    i.then_inc(s_part, 1)
            dve.wait_ge(s_hnhi, 1)
            nc.vector.tensor_tensor(h_n[:, 1], h_sb[:, :, :], h_n[:, 0].bitcast(f32), ALU.subtract).then_inc(s_hn, 1)

            for kind in range(3):
                dve.wait_ge(s_tab[kind], 16)
                step(nc.vector.tensor_reduce(peak[:, kind], tab_sb[kind], AX.X, ALU.max))
            step(nc.vector.tensor_tensor(peak[:, 0], peak[:, 0], peak[:, 1], ALU.max))
            step(nc.vector.tensor_tensor(peak[:, 0], peak[:, 0], peak[:, 2], ALU.max))
            nc.vector.tensor_scalar(peak[:, 3], peak[:, 0], -1.0, None, ALU.mult).then_inc(s_peak, 1)
            for kind in range(3):
                dve.wait_ge(s_exp, kind + 1)
                step(nc.vector.tensor_tensor(tab_sb[kind], tab_sb[kind], counts[:, kind], ALU.mult))
            step(nc.vector.tensor_tensor(att, tab_sb[0], tab_sb[1], ALU.add))
            step(nc.vector.tensor_tensor(att, att, tab_sb[2], ALU.add))
            step(nc.vector.tensor_reduce(den[:, 0], att, AX.X, ALU.add))
            step(nc.vector.tensor_scalar(den[:, 0], den[:, 0], TINY, None, ALU.max))
            step(nc.vector.reciprocal(den[:, 1], den[:, 0]))
            for b in range(NB):
                nc.vector.tensor_scalar(att[:, b], att[:, b], den[:, 1, b:b + 1], None, ALU.mult).then_inc(s_att, 1)
            for b in range(NB):
                dve.wait_ge(s_athi, b + 1)
                nc.vector.tensor_tensor(att_t[:, 1, b], bank[b][:, :], att_t[:, 0, b].bitcast(f32), ALU.subtract
                                        ).then_inc(s_atlo, 1)
            for k in range(KT):
                dve.wait_ge(s_zhi, k + 1)
                nc.vector.tensor_tensor(z_t[:, 1, k], bank[(k + 4) % 8][:, :], z_t[:, 0, k].bitcast(f32), ALU.subtract
                                        ).then_inc(s_zlo, 1)
            dve.wait_ge(s_xre, 32)

            def finish(half):
                cols = slice(half * HALF, (half + 1) * HALF)
                dve.wait_ge(s_wused, PH_BOT + 4 * half + 4)
                for b in range(NB):
                    step(nc.vector.tensor_tensor(partial[:, b, cols], partial[:, b, cols], bank[4 * half + b][:, :],
                                                 ALU.add))
                    nc.vector.scalar_tensor_tensor(out=partial[:, b, cols], in0=partial[:, b, cols], scalar=0.0,
                                                   in1=stage[:, half, b], op0=ALU.max, op1=ALU.add).then_inc(s_out, 1)

            for c in range(34, 38):
                split_lo(c)
            finish(0)
            for c in range(38, CHUNKS):
                split_lo(c)
            finish(1)

        @block.tensor
        def _(pe):
            def products(to, hi, lo, slot, k, first, last):
                nc.tensor.matmul(to, hi, w_hi[:, slot, k], start=first, stop=False)
                nc.tensor.matmul(to, hi, w_lo[:, slot, k], start=False, stop=False)
                return nc.tensor.matmul(to, lo, w_hi[:, slot, k], start=False, stop=last)

            pe.wait_ge(s_iota, 1)
            for b in range(NB):
                pe.wait_ge(s_h, b + 1)
                for k in range(KT):
                    i = nc.tensor.transpose(bank[k][:, b * P:(b + 1) * P], h_sb[:, b, k * P:(k + 1) * P], ident[:, :])
                    if b == NB - 1:
                        i.then_inc(s_tr, 1)
            pe.wait_ge(s_tlo, KT)

            def node_products(base, body, i):
                for j in range(4):
                    pe.wait_ge(s_wlo, base + 4 * i + (j + 1))
                    if j == 0:
                        pe.wait_ge(s_pev, 1 + body + i)
                    if j == 2:
                        pe.wait_ge(s_qev, 1 + body + i)
                    for k in range(KC):
                        kk = KC * (j % 2) + k
                        for b in range(NB):
                            m = products(bank[4 * (j // 2) + b][:, :], h_t[:, 0, kk, b * P:(b + 1) * P],
                                         h_t[:, 1, kk, b * P:(b + 1) * P], j % SPLIT, k, kk == 0, kk == KT - 1)
                    m.then_inc(s_wused, 1)

            with pe.Fori(0, NHALF) as i:
                node_products(PH_HO, 0, i)
            pe.wait_ge(s_hh_rows, 64)
            pe.wait_ge(s_pev, 3)
            pe.wait_ge(s_qev, 3)
            for k in range(KT):
                for j in range(2):
                    side, kk = divmod(2 * k + j, KT)
                    for e in range(T_HH):
                        i = nc.tensor.transpose(bank[k][:, (2 * j + e) * P:(2 * j + e + 1) * P],
                                                hh_rows[:, 2 * side + e, kk * P:(kk + 1) * P], ident[:, :])
                i.then_inc(s_tr, 1)
            pe.wait_ge(s_tlo, 2 * KT)

            def open_counts(banks, start):
                for b in range(NB):
                    i = nc.tensor.matmul(bank[banks + b][:, :], zeros[:, :], node_row[:, :], start=start, stop=not start)
                return i

            def count_group(g, slot, banks):
                pe.wait_ge(s_one, g + 1)
                for j in range(2):
                    for b in range(NB):
                        i = nc.tensor.matmul(bank[banks + b][:, :], onehot[:, slot, j, 1, b * P:(b + 1) * P],
                                             onehot[:, slot, j, 0], start=False, stop=False)
                i.then_inc(s_oused, 1)

            open_counts(0, True)
            with pe.Fori(0, T_HO // 4) as i:
                for j in range(2):
                    count_group(2 * i + j, j, 0)
            open_counts(0, False).then_inc(s_cnt, 1)
            open_counts(4, True)
            for g in range(T_HO // 2, T_NODE // 2):
                count_group(g, g % 2, 4)
            open_counts(4, False).then_inc(s_cnt, 1)
            pe.wait_ge(s_cev, 1)
            open_counts(0, True)
            count_group(T_NODE // 2, (T_NODE // 2) % 2, 0)
            open_counts(0, False).then_inc(s_cnt, 1)
            pe.wait_ge(s_cev, 3)

            with pe.Fori(0, NHALF) as i:
                node_products(PH_OO, 2, i)
            pe.wait_ge(s_pev, 5)
            pe.wait_ge(s_qev, 5)
            for half in range(NHALF):
                for j in range(4):
                    pe.wait_ge(s_wlo, PH_HH + 4 * half + j + 1)
                    for k in range(KC):
                        kk = KC * j + k
                        for e in range(T_HH):
                            m = products(bank[4 * half + e][:, :], feat_hi[:, kk, e * P:(e + 1) * P],
                                         feat_lo[:, kk, e * P:(e + 1) * P], j % SPLIT, k, kk == 0, kk == 2 * KT - 1)
                    m.then_inc(s_wused, 1)

            def last_product(phase, hi_lo, half):
                for j in range(4):
                    pe.wait_ge(s_wlo, phase + 4 * half + j + 1)
                    for k in range(KC):
                        kk = KC * (j % 2) + k
                        for b in (range(0, 1) if j < 2 else range(1, NB)):
                            m = products(bank[4 * half + b][:, :], hi_lo[:, 0, kk, b * P:(b + 1) * P],
                                         hi_lo[:, 1, kk, b * P:(b + 1) * P], j % SPLIT, k, kk == 0, kk == KT - 1)
                    m.then_inc(s_wused, 1)

            for half in range(NHALF):
                pe.wait_ge(s_hhev, half + 1)
                last_product(PH_TOP, h_t, half)
            pe.wait_ge(s_part, 2)
            for a in range(NB):
                pe.wait_ge(s_att, NB)
                for b in range(NB):
                    i = nc.tensor.transpose(bank[a][:, b * P:(b + 1) * P], att[:, b, a * P:(a + 1) * P], ident[:, :])
                i.then_inc(s_attr, 1)
            pe.wait_ge(s_hn, 1)
            pe.wait_ge(s_atlo, NB)
            for k in range(KT):
                to = bank[(k + 4) % 8][:, :]
                for a in range(NB):
                    hi, lo = h_n[:, 0, a, k * P:(k + 1) * P], h_n[:, 1, a, k * P:(k + 1) * P]
                    nc.tensor.matmul(to, hi, att_t[:, 0, a], start=a == 0, stop=False)
                    nc.tensor.matmul(to, hi, att_t[:, 1, a], start=False, stop=False)
                    i = nc.tensor.matmul(to, lo, att_t[:, 0, a], start=False, stop=a == NB - 1)
                i.then_inc(s_z, 1)
            pe.wait_ge(s_zlo, KT)
            for half in range(NHALF):
                last_product(PH_BOT, z_t, half)

        @block.gpsimd
        def _(pool):
            nc.gpsimd.memset(stage[:, 0], EMPTY).then_inc(s_empty, 1)
            nc.gpsimd.memset(ident[:, :], 0.0)
            nc.gpsimd.memset(zeros[:, :], 0.0)
            nc.gpsimd.iota(node_row[:, :], [[1, N]], base=0, channel_multiplier=0,
                           allow_small_or_imprecise_dtypes=True).then_inc(s_now, 1)
            pool.wait_ge(s_now, 1)
            nc.gpsimd.affine_select(out=ident[:, :], in_=ident[:, :], compare_op=ALU.not_equal, fill=1.0, base=0,
                                    pattern=[[-1, P]], channel_multiplier=1).then_inc(s_iota, 1)

            def gather(to, table, nodes, landed):
                nc.gpsimd.indirect_dma_start(to, None, table[:, :], bass.IndirectOffsetOnAxis(ap=nodes, axis=0)
                                             ).then_inc(landed, 16)

            pool.wait_ge(s_index, 1)
            pool.wait_ge(s_hd, 16)
            for side, nodes in ((0, i_src), (1, i_dst)):
                for e in range(T_HH):
                    gather(hh_rows[:, 2 * side + e], h_dram, nodes[:, T_NODE + e:T_NODE + e + 1], s_hh_rows)

            def wait(what, value):
                pool.wait_ge(what, value)
                pool.sem_inc(s_turn, 1)

            def take(t, row, s):
                nc.gpsimd.tensor_copy(index_now[:, s], row).then_inc(s_now, 1)
                wait(s_now, t + 2)

            def gather_tile(kind, s):
                tab_p, tab_q = node_tab[kind]
                gather(edge_p[:, s], tab_p, index_now[:, s, 0:1], s_gath[s])
                gather(edge_q[:, s], tab_q, index_now[:, s, 1:2], s_gath[s])

            def finish_logit(s):
                nc.gpsimd.tensor_scalar(logit_out[:, s:s + 1], logit[:, s:s + 1], ba[:, 0:1], None, ALU.add)

            def scatter(kind, s):
                nc.gpsimd.indirect_dma_start(pair_tab[kind][:, :], bass.IndirectOffsetOnAxis(ap=index_now[:, s, 2:3], axis=0),
                                             logit_out[:, s:s + 1], None).then_inc(s_scat, 16)

            pool.wait_ge(s_const, 32)
            pool.wait_ge(s_tabs, 48)
            pool.wait_ge(s_pst, 32)
            pool.wait_ge(s_qst, 32)
            pool.wait_ge(s_tr, 2 * KT)
            def next_tile(t, row, s, first=False):
                wait(s_logit, t + (1 - SLOTS))
                finish_logit(s)
                take(t, row, s)
                gather_tile("ho", s)
                if not first:
                    wait(s_scat, 16 * t - 16 * SLOTS)
                scatter("ho", s)

            for t in range(SLOTS):
                take(t, index[:, t], t)
                gather_tile("ho", t)
            for t in range(SLOTS, 2 * SLOTS):
                next_tile(t, index[:, t], t % SLOTS, first=t == SLOTS)
            with pool.Fori(2, T_HO // SLOTS) as i:
                for s in range(SLOTS):
                    next_tile(SLOTS * i + s, index[:, bass.ds(SLOTS * i + s, 1)].rearrange("p o c -> p (o c)"), s)
            for t in range(T_HO, T_NODE + SLOTS):
                s = t % SLOTS
                pool.wait_ge(s_logit, t - SLOTS + 1)
                finish_logit(s)
                take(t, index[:, t], s)
                if t == T_HO:
                    pool.wait_ge(s_pst, 64)
                    pool.wait_ge(s_qst, 64)
                if t < T_NODE:
                    gather_tile("oo", s)
                pool.wait_ge(s_scat, 16 * (t - SLOTS))
                scatter("ho" if t - SLOTS < T_HO else "oo", s)
                if t == T_HO + SLOTS + 1:
                    pool.wait_ge(s_hhlog, 1)
                    nc.gpsimd.tensor_scalar(logit_hh_out[:, :], logit_hh[:, :], ba[:, 0:1], None, ALU.add
                                            ).then_inc(s_hhout, 1)
                    pool.wait_ge(s_hhout, 1)
                    for e in range(T_HH):
                        if e:
                            pool.wait_ge(s_hhscat, 16 * e)
                        nc.gpsimd.indirect_dma_start(pair_tab["hh"][:, :],
                                                     bass.IndirectOffsetOnAxis(ap=pair_hh[:, e:e + 1], axis=0),
                                                     logit_hh_out[:, e:e + 1], None).then_inc(s_hhscat, 16)
            pool.wait_ge(s_logit, T_NODE)
            for kind, name in enumerate(("ho", "oo", "hh")):
                if name == "ho":
                    pool.wait_ge(s_scat, 16 * T_HO)
                if name == "oo":
                    pool.wait_ge(s_scat, 16 * T_NODE)
                if name == "hh":
                    pool.wait_ge(s_hhscat, 16 * T_HH)
                pool.dma_start(tab_sb[kind], pair_tab[name].rearrange("(b p n) o -> p b (n o)", p=P, n=N)
                               ).then_inc(s_tab[kind], 16)


def kernel(x, src, dst, L0_gnn_W_hh, L0_gnn_b_hh, L0_gnn_W_oo, L0_gnn_b_oo, L0_gnn_W_ho, L0_gnn_b_ho,
           L0_gnn_W_a, L0_gnn_b_a, L0_gnn_W_hn, L0_gnn_b_hn, L0_gnn_W_on, L0_gnn_b_on):
    import numpy as np
    import concourse.bacc as bacc
    from concourse.bass_utils import run_bass_kernel_spmd

    def chunks(w, first, n, half):
        w = np.asarray(w).reshape(2 * KT, P, NHALF, HALF)[first:first + n * KC, :, half]
        return w.reshape(n, KC, P, HALF).transpose(0, 2, 1, 3)

    order = [chunks(w, 0, 4, half) for w in (L0_gnn_W_ho, L0_gnn_W_oo, L0_gnn_W_hh) for half in range(NHALF)]
    order += [chunks(w, first, 2, half) for first in (0, KT) for half in range(NHALF)
              for w in (L0_gnn_W_hn, L0_gnn_W_on)]
    arrays = {
        "x": np.ascontiguousarray(x), "src": np.ascontiguousarray(src), "dst": np.ascontiguousarray(dst),
        "w_chunks": np.ascontiguousarray(np.concatenate(order)),
        "biases": np.stack([np.asarray(b) for b in (L0_gnn_b_ho, L0_gnn_b_oo, L0_gnn_b_hh, L0_gnn_b_hn, L0_gnn_b_on)]),
        "w_a": np.ascontiguousarray(np.asarray(L0_gnn_W_a).reshape(1, D)),
        "b_a": np.ascontiguousarray(np.asarray(L0_gnn_b_a).reshape(1, 1)),
    }
    nc = bacc.Bacc("TRN2", target_bir_lowering=False, num_devices=1)
    args = [nc.dram_tensor(name, a.shape, mybir.dt.from_np(a.dtype), kind="ExternalInput").ap()
            for name, a in arrays.items()]
    out = nc.dram_tensor("out", (N, D), mybir.dt.float32, kind="ExternalOutput").ap()
    build(nc, *args, out)
    return run_bass_kernel_spmd(nc, [arrays], core_ids=[0]).results[0]["out"]
```

```python
import concourse.bass as bass
from concourse import mybir
from contextlib import ExitStack

P = 128
N, D = 512, 1024
NB = N // P
KT = D // P
HALF = 512
NHALF = D // HALF
E_HH, E_OO = 256, 1280
E_HO = 8704 - E_HH - E_OO
T_HH, T_OO, T_HO = E_HH // P, E_OO // P, E_HO // P
T_ALL = T_HO + T_OO + T_HH
T_NODE = T_HO + T_OO
KC = 4
PH_HO, PH_OO, PH_HH, PH_TOP, PH_G = 0, 8, 16, 24, 32
CHUNKS = 40
RAW = 4
SPLIT = 2
SLOTS = 4
EMPTY = -3.0e38
TINY = 1.0e-30
EPS = 1e-5


def build(nc, x, src, dst, w_chunks, biases, w_a, b_a, out):
    f32, f32r, bf16, f16 = mybir.dt.float32, mybir.dt.float32r, mybir.dt.bfloat16, mybir.dt.float16
    i32, i16 = mybir.dt.int32, mybir.dt.int16
    ALU = mybir.AluOpType
    ACT = mybir.ActivationFunctionType
    AX = mybir.AxisListType

    def dram(name, shape):
        return nc.dram_tensor(name, shape, f32, kind="Internal").ap()

    h_dram = dram("h_dram", (N, D))
    node_tab = {"ho": (dram("p_ho", (N, D)), dram("q_ho", (N, D))),
                "oo": (dram("p_oo", (N, D)), dram("q_oo", (N, D)))}
    pair_tab = {k: dram(f"pairs_{k}", (N * N, 1)) for k in ("ho", "oo", "hh")}

    with ExitStack() as ctx:
        def sb(name, shape, dt):
            return ctx.enter_context(nc.sbuf_tensor(name, shape, dt))

        def shared(*specs):
            got = []
            for spec in specs[:-1]:
                with nc.sbuf_tensor(*spec) as t:
                    got.append(t)
            return got + [sb(*specs[-1])]

        def sem(name):
            return ctx.enter_context(nc.semaphore(name))

        h_t = sb("h_t", [P, 2, KT, N], f32r)
        raw = sb("raw", [P, RAW, KC, HALF], f32)
        w_hi = sb("w_hi", [P, SPLIT, KC, HALF], f32r)
        w_lo = sb("w_lo", [P, SPLIT, KC, HALF], f32r)
        g_hi = [h_t[:, n, :, :].rearrange("p (f b) n -> p f b n", f=NHALF) for n in range(2)]
        g_lo = [w_hi[:, :], w_lo[:, :]]
        gath = sb("gath", [P, 2, SLOTS, D], f32)
        feat_hi, partial = shared(("feat_hi", [P, 2 * KT, E_HH], f32r), ("partial", [P, NB, D], f32))
        feat_lo, att_t, g_on, h_sb = shared(("feat_lo", [P, 2 * KT, E_HH], f32r), ("att_t", [P, 2, NB, N], f32r),
                                            ("g_on", [P, NHALF, NB, HALF], f32), ("h_sb", [P, NB, D], f32))
        count_buf, stage = shared(("count_buf", [P, 2, NB, 2, N], bf16), ("stage", [P, 2, NB, HALF], f32))
        rows = count_buf[:, 0].rearrange("p (g j) s n -> p g j s n", g=2)
        step_sums = count_buf[:, 1].rearrange("p b k n -> p k b n").bitcast(i16)
        counts = sb("counts", [P, 3, NB, N], i16)
        g_hn, bias = shared(("g_hn", [P, NB, HALF], f32), ("bias", [P, 2, D], f32))
        wa = sb("wa", [P, D], f32)
        ba = sb("ba", [P, 1], f32)
        ident = sb("ident", [P, P], f32)
        zeros = sb("zeros", [P, P], f16)
        node_row = sb("node_row", [P, N], f16)
        i_src = sb("i_src", [P, T_ALL], i32)
        i_dst = sb("i_dst", [P, T_ALL], i32)
        f_src = sb("f_src", [P, T_ALL], f32)
        step_at = sb("step_at", [P, T_ALL], f32)
        f_dst = sb("f_dst", [P, T_ALL], f32)
        index = sb("index", [P, T_NODE + SLOTS, 4], i32)
        index_f = index[:, :, :].bitcast(f32)
        pair_hh = sb("pair_hh", [P, T_HH], i32)
        index_now = sb("index_now", [P, SLOTS, 4], i32)
        logit_half = sb("logit_half", [P, NHALF, T_HH], f32)
        logit_hh = sb("logit_hh", [P, T_HH], f32)
        stats = sb("stats", [P, NB, 2, 6], f32)
        mv = sb("mv", [P, NB, 2], f32)
        rstd = sb("rstd", [P, 4, NB], f32)
        peak = sb("peak", [P, 8, NB], f32)
        den = sb("den", [P, 2, NB], f32)

        edge_p, edge_q = gath[:, 0], gath[:, 1]
        x_sb = gath[:, 0]
        hh_rows = gath[:, 1]
        tab_sb = [stage[:, 0], gath[:, 0, 0:2, :].rearrange("p a (b n) -> p (a b) n", n=N), stage[:, 1]]
        att = gath[:, 1, 2:4, :].rearrange("p a (b n) -> p (a b) n", n=N)
        bank = [ctx.enter_context(nc.psum_tensor(f"bank{i}", [P, HALF], f32)) for i in range(8)]

        s_x = [sem(f"x_landed{b}") for b in range(NB)]
        s_idx, s_const, s_bias, s_tabs = sem("indices_landed"), sem("constants_landed"), sem("bias_landed"), sem("pair_tables_cleared")
        s_empty, s_iota, s_index = sem("empty_ready"), sem("iota_ready"), sem("index_ready")
        s_var, s_std, s_norm, s_h = sem("variance_ready"), sem("std_ready"), sem("norm_ready"), sem("h_ready")
        s_hd, s_hh_rows = sem("h_stored"), sem("hh_rows_landed")
        s_tr, s_thi, s_tlo = sem("transposed"), sem("transposed_hi"), sem("transposed_lo")
        s_raw = [sem(f"raw_landed{i}") for i in range(RAW)]
        s_whi, s_wlo, s_wused = sem("weights_hi"), sem("weights_lo"), sem("weights_used")
        s_pev, s_qev = sem("p_evacuated"), sem("q_evacuated")
        s_pst, s_qst = sem("p_stored"), sem("q_stored")
        s_steps, s_diff = sem("src_steps_ready"), sem("counts_ready")
        s_one, s_oused, s_cnt, s_cev = sem("onehot_ready"), sem("onehot_used"), sem("counted"), sem("counts_evacuated")
        s_gath = [sem(f"edge_rows_landed{i}") for i in range(SLOTS)]
        s_now, s_esum, s_logit, s_scat = sem("index_now_ready"), sem("edge_summed"), sem("logit_ready"), sem("logits_scattered")
        s_hhlog, s_hhscat = sem("hh_logits_ready"), sem("hh_scattered")
        s_hhev, s_hhhalf = sem("hh_evacuated"), sem("hh_half_logits")
        s_part = sem("partial_ready")
        s_xre, s_gev, s_ghi, s_glo = sem("x_reloaded"), sem("g_evacuated"), sem("g_hi_ready"), sem("g_lo_ready")
        s_tab = [sem(f"table_loaded_{kind}") for kind in pair_tab]
        s_peak, s_exp, s_att, s_attr = sem("peak_ready"), sem("exp_ready"), sem("att_ready"), sem("att_transposed")
        s_athi, s_atlo, s_den = sem("att_hi"), sem("att_lo"), sem("sums_inverted")
        s_fin, s_out, s_stored = sem("product_ready"), sem("out_ready"), sem("out_stored")
        s_dve, s_turn = sem("vector_step"), sem("pool_turns")

        block = ctx.enter_context(nc.Block())

        def blocks(t):
            return t.rearrange("(b p) d -> p b d", p=P)

        @block.sync
        def _(sp):
            for b in range(NB):
                sp.dma_start(x_sb[:, b], x[b * P:(b + 1) * P, :]).then_inc(s_x[b], 16)
            for c in range(RAW):
                sp.dma_start(raw[:, c], w_chunks[c]).then_inc(s_raw[c], 16)
            sp.wait_ge(s_h, NB)
            sp.dma_start(blocks(h_dram), h_sb[:, :, :]).then_inc(s_hd, 16)
            with sp.Fori(1, CHUNKS // RAW) as i:
                for s in range(RAW):
                    sp.wait_ge(s_wlo, RAW * i + (s + 1 - RAW))
                    sp.dma_start(raw[:, s], w_chunks[bass.ds(RAW * i + s, 1)].rearrange("o p k n -> (o p) k n")
                                 ).then_inc(s_raw[s], 16)
            for n in range(NB * NHALF):
                b, half = divmod(n, NHALF)
                sp.wait_ge(s_out, n + 1)
                sp.dma_start(out[b * P:(b + 1) * P, half * HALF:(half + 1) * HALF],
                             partial[:, b, half * HALF:(half + 1) * HALF]).then_inc(s_stored, 16)
            sp.wait_ge(s_stored, 16 * NB * NHALF)

        @block.scalar
        def _(act):
            for t0, tiles, e0 in ((0, T_HO, E_HH + E_OO), (T_HO, T_OO, E_HH), (T_NODE, T_HH, 0)):
                for to, of in ((i_src, src), (i_dst, dst)):
                    act.dma_start(to[:, t0:t0 + tiles], of[e0:e0 + tiles * P].rearrange("(p t) -> p t", p=P)
                                  ).then_inc(s_idx, 16)
            act.dma_start(wa[:, :], w_a.to_broadcast((P, D))).then_inc(s_const, 16)
            act.dma_start(ba[:, :], b_a.to_broadcast((P, 1))).then_inc(s_const, 16)
            for n in range(2):
                act.dma_start(bias[:, n], biases[n:n + 1, :].to_broadcast((P, D))).then_inc(s_bias, 16)

            for b in range(NB):
                act.wait_ge(s_var, b + 1)
                nc.scalar.activation(rstd[:, 1, b:b + 1], rstd[:, 0, b:b + 1], ACT.Sqrt).then_inc(s_std, 1)
            for b in range(NB):
                act.wait_ge(s_norm, b + 1)
                nc.scalar.activation(h_sb[:, b], x_sb[:, b], ACT.Relu, bias=rstd[:, 3, b:b + 1],
                                     scale=rstd[:, 2, b:b + 1]).then_inc(s_h, 1)
            act.wait_ge(s_empty, 1)
            for t in pair_tab.values():
                act.dma_start(t.rearrange("(p n) o -> p (n o)", p=P), stage[:, 0].rearrange("p b n -> p (b n)")
                              ).then_inc(s_tabs, 16)
            for k in range(KT):
                act.wait_ge(s_tr, k + 1)
                nc.scalar.activation(h_t[:, 0, k], bank[k][:, :], ACT.Copy).then_inc(s_thi, 1)
            act.sem_inc(s_qev, 1)

            def split_hi(c):
                act.wait_ge(s_raw[c % RAW], 16 * (c // RAW + 1))
                if c >= SPLIT:
                    act.wait_ge(s_wused, c - SPLIT + 1)
                nc.scalar.activation(w_hi[:, c % SPLIT], raw[:, c % RAW], ACT.Copy).then_inc(s_whi, 1)

            def store_half(tab, half, side):
                act.dma_start(blocks(tab)[:, :, half * HALF:(half + 1) * HALF], stage[:, side]
                              ).then_inc((s_pst, s_qst)[side], 16)

            def store_p(n, kind):
                act.wait_ge(s_pev, n + 2)
                store_half(node_tab[kind][0], n % 2, 0)

            def evacuate_q(n, kind):
                act.wait_ge(s_wused, 4 * (n + 1))
                if n:
                    act.wait_ge(s_qst, 16 * n)
                else:
                    act.wait_ge(s_tabs, 48)
                for b in range(NB):
                    i = nc.scalar.activation(stage[:, 1, b], bank[4 + b][:, :], ACT.Copy)
                i.then_inc(s_qev, 1)
                act.wait_ge(s_qev, n + 2)
                store_half(node_tab[kind][1], n % 2, 1)

            for c in range(4):
                split_hi(c)
            store_p(0, "ho")
            split_hi(4)
            split_hi(5)
            evacuate_q(0, "ho")
            split_hi(6)
            split_hi(7)
            store_p(1, "ho")
            act.dma_start(bias[:, 0], biases[2:3, :].to_broadcast((P, D))).then_inc(s_bias, 16)
            split_hi(8)
            evacuate_q(1, "ho")
            for k in range(KT):
                act.wait_ge(s_tr, KT + k + 1)
                nc.scalar.activation(feat_hi[:, 2 * k:2 * k + 2].rearrange("p k e -> p (k e)"), bank[k][:, :], ACT.Copy
                                     ).then_inc(s_thi, 1)
            split_hi(9)

            def src_steps(g, slot, used):
                if used is not None:
                    act.wait_ge(s_oused, used)
                for j in range(2):
                    i = nc.scalar.activation(rows[:, slot, j, 0], node_row[:, :], ACT.Sign,
                                             bias=step_at[:, bass.ds(2 * g + j, 1)])
                i.then_inc(s_steps, 1)

            def evacuate_sums(kind, banks, slot):
                act.wait_ge(s_cnt, kind + 1)
                if kind >= 2:
                    act.wait_ge(s_diff, kind - 1)
                for b in range(NB):
                    i = nc.scalar.activation(step_sums[:, slot, b], bank[banks + b][:, :], ACT.Copy)
                i.then_inc(s_cev, 1)

            act.wait_ge(s_index, 1)
            act.wait_ge(s_iota, 1)
            act.wait_ge(s_pst, 32)
            act.wait_ge(s_qst, 32)
            src_steps(0, 0, None)
            src_steps(1, 1, None)
            with act.Fori(1, T_HO // 4) as i:
                for j in range(2):
                    src_steps(2 * i + j, j, 2 * i + (j - 1))
            for g in range(T_HO // 2, T_ALL // 2):
                src_steps(g, g % 2, g - 1)
            evacuate_sums(0, 0, 0)
            evacuate_sums(1, 4, 1)
            evacuate_sums(2, 0, 0)
            for n in (2, 3):
                split_hi(4 * n + 2)
                split_hi(4 * n + 3)
                store_p(n, "oo")
                split_hi(4 * n + 4)
                evacuate_q(n, "oo")
                split_hi(4 * n + 5)
            for c in range(18, 26):
                split_hi(c)
            act.wait_ge(s_hhlog, 1)
            for n in range(2):
                act.dma_start(bias[:, n], biases[3 + n:4 + n, :].to_broadcast((P, D))).then_inc(s_bias, 16)
            for c in range(26, 36):
                split_hi(c)

            def evacuate_g(q, to):
                act.wait_ge(s_wused, PH_G + 2 * q + 2)
                for b in range(NB):
                    i = nc.scalar.activation(to[:, b], bank[4 * (q % 2) + b][:, :], ACT.Copy)
                i.then_inc(s_gev, 1)

            evacuate_g(0, g_on[:, 0])
            split_hi(36)
            split_hi(37)
            evacuate_g(1, g_on[:, 1])
            split_hi(38)
            split_hi(39)
            act.wait_ge(s_part, 2)
            evacuate_g(2, g_hn)

            def exps(kind, ready, bias_at):
                act.wait_ge(s_peak, ready)
                for b in range(NB):
                    nc.scalar.activation(tab_sb[kind][:, b], tab_sb[kind][:, b], ACT.Exp,
                                         bias=peak[:, bias_at, b:b + 1]).then_inc(s_exp, 1)

            exps(0, 1, 4)
            exps(2, 1, 4)
            act.wait_ge(s_wused, CHUNKS)
            act.wait_ge(s_gev, 3)
            nc.scalar.activation(g_hi[0], g_on[:, :], ACT.Copy).then_inc(s_ghi, 1)
            nc.scalar.activation(g_hi[1][:, 0], g_hn[:, :], ACT.Copy).then_inc(s_ghi, 1)
            for b in range(NB):
                i = nc.scalar.activation(g_hi[1][:, 1, b], bank[4 + b][:, :], ACT.Copy)
            i.then_inc(s_ghi, 1)
            act.wait_ge(s_peak, 2)
            nc.scalar.activation(peak[:, 7], peak[:, 6], ACT.Exp).then_inc(s_exp, 1)
            exps(1, 2, 5)
            act.wait_ge(s_wlo, CHUNKS)
            for half in range(NHALF):
                act.dma_start(raw[:, half], blocks(x)[:, :, half * HALF:(half + 1) * HALF]).then_inc(s_xre, 16)
            for b in range(NB):
                act.wait_ge(s_attr, b + 1)
                if b == 0:
                    act.wait_ge(s_glo, 1)
                nc.scalar.activation(att_t[:, 0, b], bank[b][:, :], ACT.Copy).then_inc(s_athi, 1)

        @block.vector
        def _(dve):
            steps = [0]

            def step(i):
                steps[0] += 1
                i.then_inc(s_dve, 1)
                dve.wait_ge(s_dve, steps[0])

            for b in range(NB):
                dve.wait_ge(s_x[b], 16)
                for j in range(2):
                    i = nc.vector.bn_stats(stats[:, b, j], x_sb[:, b, j * HALF:(j + 1) * HALF])
                step(i)
                step(nc.vector.bn_aggr(mv[:, b], stats[:, b]))
                nc.vector.tensor_scalar(rstd[:, 0, b:b + 1], mv[:, b, 1:2], EPS, None, ALU.add).then_inc(s_var, 1)
            for b in range(NB):
                dve.wait_ge(s_std, b + 1)
                var, half, r = (rstd[:, n, b:b + 1] for n in range(3))
                step(nc.vector.reciprocal(r, half))
                step(nc.vector.tensor_scalar(half, r, r, var, ALU.mult, ALU.mult))
                step(nc.vector.tensor_scalar(half, half, -0.5, 1.5, ALU.mult, ALU.add))
                step(nc.vector.tensor_scalar(r, r, half, None, ALU.mult))
                nc.vector.tensor_scalar(rstd[:, 3, b:b + 1], mv[:, b, 0:1], r, -1.0, ALU.mult, ALU.mult
                                        ).then_inc(s_norm, 1)
            dve.wait_ge(s_idx, 16 * 6)
            step(nc.vector.memset(index[:, :, :], 0))
            nc.vector.tensor_copy(f_src[:, :], i_src[:, :])
            nc.vector.tensor_copy(f_dst[:, :], i_dst[:, :])
            step(nc.vector.tensor_copy(index[:, 0:T_NODE, 0], i_src[:, 0:T_NODE]))
            nc.vector.tensor_copy(index[:, 0:T_NODE, 1], i_dst[:, 0:T_NODE])
            nc.vector.tensor_scalar(step_at[:, :], f_src[:, :], -1.0, 0.5, ALU.mult, ALU.add)
            nc.vector.scalar_tensor_tensor(out=index[:, SLOTS:SLOTS + T_NODE, 2], in0=f_dst[:, 0:T_NODE],
                                           scalar=float(N), in1=f_src[:, 0:T_NODE], op0=ALU.mult, op1=ALU.add)
            nc.vector.scalar_tensor_tensor(out=pair_hh[:, :], in0=f_dst[:, T_NODE:T_ALL], scalar=float(N),
                                           in1=f_src[:, T_NODE:T_ALL], op0=ALU.mult, op1=ALU.add).then_inc(s_index, 1)
            for k in range(KT):
                dve.wait_ge(s_thi, k + 1)
                nc.vector.tensor_tensor(h_t[:, 1, k], bank[k][:, :], h_t[:, 0, k].bitcast(f32), ALU.subtract
                                        ).then_inc(s_tlo, 1)

            def split_lo(c, slot=None):
                slot = c if slot is None else slot
                dve.wait_ge(s_whi, c + 1)
                nc.vector.tensor_tensor(w_lo[:, slot % SPLIT], raw[:, slot % RAW],
                                        w_hi[:, slot % SPLIT].bitcast(f32), ALU.subtract).then_inc(s_wlo, 1)

            def evacuate_p(n, half, slot):
                dve.wait_ge(s_wused, 4 * n + 2)
                for b in range(NB):
                    i = nc.vector.tensor_tensor(stage[:, 0, b], bank[b][:, :], bias[:, slot, bass.ds(half * HALF, HALF)],
                                                ALU.add)
                i.then_inc(s_pev, 1)

            def edge_logit(p, q, t):
                dve.wait_ge(s_esum, t + 1)
                nc.vector.scalar_tensor_tensor(out=q, in0=p, scalar=0.0, in1=wa[:, :], op0=ALU.max, op1=ALU.mult,
                                               accum_out=index_f[:, bass.ds(t + SLOTS, 1), 3]).then_inc(s_logit, 1)

            def edges(n, t, s, landed):
                for j in range(n):
                    slot = (s + j) % SLOTS
                    dve.wait_ge(s_gath[slot], landed + 32 * ((s + j) // SLOTS))
                    p, q = edge_p[:, slot], edge_q[:, slot]
                    nc.vector.tensor_tensor(p, p, q, ALU.add).then_inc(s_esum, 1)
                    edge_logit(p, q, t + j)

            dve.sem_inc(s_pev, 1)
            for c in range(4):
                split_lo(c)
            dve.wait_ge(s_bias, 32)
            dve.wait_ge(s_tabs, 48)
            evacuate_p(0, 0, 0)
            for c in range(4, 8):
                split_lo(c)
            dve.wait_ge(s_pst, 16)
            evacuate_p(1, 1, 0)
            split_lo(8)
            for k in range(KT):
                dve.wait_ge(s_thi, KT + k + 1)
                nc.vector.tensor_tensor(feat_lo[:, 2 * k:2 * k + 2].rearrange("p k e -> p (k e)"), bank[k][:, :],
                                        feat_hi[:, 2 * k:2 * k + 2].rearrange("p k e -> p (k e)").bitcast(f32),
                                        ALU.subtract).then_inc(s_tlo, 1)
            split_lo(9)
            dve.wait_ge(s_const, 32)
            dve.wait_ge(s_iota, 1)
            dve.wait_ge(s_pst, 32)
            dve.wait_ge(s_qst, 32)

            def one_hot(g, slot, used):
                if used is not None:
                    dve.wait_ge(s_oused, used)
                for j in range(2):
                    i = nc.vector.tensor_scalar(rows[:, slot, j, 1], node_row[:, :],
                                                f_dst[:, bass.ds(2 * g + j, 1)], None, ALU.is_equal)
                i.then_inc(s_one, 1)

            def difference(n, kind, slot):
                dve.wait_ge(s_cev, n)
                sums = step_sums[:, slot]
                nc.vector.tensor_tensor(counts[:, kind, :, 1:N], sums[:, :, 1:N], sums[:, :, 0:N - 1], ALU.subtract)
                nc.vector.tensor_tensor(counts[:, kind, :, 0:1], sums[:, :, 0:1], sums[:, :, N - 1:N], ALU.add
                                        ).then_inc(s_diff, 1)

            one_hot(0, 0, None)
            one_hot(1, 1, None)
            with dve.Fori(0, 4) as i:
                for s in range(SLOTS):
                    for j in range(2):
                        one_hot(8 * i + 2 * s + j + 2, j, 8 * i + 2 * s + j + 1)
                    edges(1, 4 * i + s, s, 32 * i + 32)
            for n, kind in enumerate((0, 1, 2)):
                difference(n + 1, kind, n % 2)
            with dve.Fori(0, 2) as i:
                for j in range(4):
                    edges(2, 16 + 8 * i + 2 * j, (2 * j) % SLOTS, 32 * (4 + 2 * i + 2 * j // SLOTS) + 32)
                    split_lo(10 + 4 * i + j, 10 + j)
                    if j == 1:
                        dve.wait_ge(s_pst, 32 + 16 * i)
                        dve.wait_ge(s_oused, 34)
                        evacuate_p(2 + i, i, 1)
            for half in range(NHALF):
                for j in range(4):
                    c = 18 + 4 * half + j
                    t = 32 + 4 * half + j
                    edges(1, t, t % SLOTS, 32 * (t // SLOTS) + 32)
                    split_lo(c)
                    if j == 3:
                        dve.wait_ge(s_bias, 48)
                        dve.wait_ge(s_pst, 64)
                        dve.wait_ge(s_qst, 64)
                        dve.wait_ge(s_wused, PH_HH + 4 * half + 4)
                        for e in range(T_HH):
                            i = nc.vector.tensor_tensor(stage[:, 0, e], bank[4 * half + e][:, :],
                                                        bias[:, 0, half * HALF:(half + 1) * HALF], ALU.add)
                        i.then_inc(s_hhev, 1)
                        dve.wait_ge(s_hhev, half + 1)
                        for e in range(T_HH):
                            i = nc.vector.scalar_tensor_tensor(out=stage[:, 1, e], in0=stage[:, 0, e], scalar=0.0,
                                                               in1=wa[:, half * HALF:(half + 1) * HALF],
                                                               op0=ALU.max, op1=ALU.mult,
                                                               accum_out=logit_half[:, half, e:e + 1])
                        i.then_inc(s_hhhalf, 1)
                        dve.wait_ge(s_hhhalf, half + 1)
            nc.vector.tensor_tensor(logit_hh[:, :], logit_half[:, 0], logit_half[:, 1], ALU.add).then_inc(s_hhlog, 1)
            dve.wait_ge(s_bias, 80)
            for j in range(8):
                t = 40 + j
                edges(1, t, t % SLOTS, 32 * (t // SLOTS) + 32)
                split_lo(26 + j)
                if j in (3, 7):
                    half = j // 4
                    dve.wait_ge(s_wused, PH_TOP + 4 * half + 4)
                    for b in range(NB):
                        i = nc.vector.tensor_tensor(partial[:, b, half * HALF:(half + 1) * HALF], bank[4 * half + b][:, :],
                                                    bias[:, min(b, 1), half * HALF:(half + 1) * HALF], ALU.add)
                    i.then_inc(s_part, 1)
            t = 48
            for j in range(7):
                n = 3 if j in (0, 4) else 2
                edges(n, t, t % SLOTS, 32 * (t // SLOTS) + 32)
                t += n
                if j < 6:
                    split_lo(34 + j)
            pk_ho, pk_hh, m1, m, bias1, bias2, drop, drop_exp = (peak[:, n] for n in range(8))
            for kind, to in ((0, pk_ho), (2, pk_hh)):
                dve.wait_ge(s_tab[kind], 16)
                i = nc.vector.tensor_reduce(to, tab_sb[kind], AX.X, ALU.max)
            step(i)
            step(nc.vector.tensor_tensor(m1, pk_ho, pk_hh, ALU.max))
            step(nc.vector.tensor_scalar(m, m1, ba[:, 0:1], None, ALU.add))
            nc.vector.tensor_scalar(bias1, m, -1.0, ba[:, 0:1], ALU.mult, ALU.add).then_inc(s_peak, 1)
            for n, kind in enumerate((0, 2)):
                for b in range(NB):
                    dve.wait_ge(s_exp, NB * n + b + 1)
                    i = nc.vector.tensor_tensor(tab_sb[kind][:, b], tab_sb[kind][:, b], counts[:, kind, b], ALU.mult)
            step(i)
            step(nc.vector.tensor_tensor(tab_sb[0], tab_sb[0], tab_sb[2], ALU.add))
            edges(T_NODE - t, t, t % SLOTS, 32 * (t // SLOTS) + 32)
            dve.wait_ge(s_ghi, 1)
            nc.vector.tensor_tensor(g_lo[0], g_on[:, :], g_hi[0].bitcast(f32), ALU.subtract).then_inc(s_glo, 1)
            dve.wait_ge(s_ghi, 3)
            nc.vector.tensor_tensor(g_lo[1][:, 0], g_hn[:, :], g_hi[1][:, 0].bitcast(f32), ALU.subtract)
            for b in range(NB):
                i = nc.vector.tensor_tensor(g_lo[1][:, 1, b], bank[4 + b][:, :], g_hi[1][:, 1, b].bitcast(f32),
                                            ALU.subtract)
            i.then_inc(s_glo, 1)
            dve.wait_ge(s_tab[1], 16)
            step(nc.vector.tensor_reduce(pk_ho, tab_sb[1], AX.X, ALU.max))
            step(nc.vector.tensor_tensor(m, m1, pk_ho, ALU.max))
            nc.vector.tensor_tensor(drop, m1, m, ALU.subtract)
            step(nc.vector.tensor_scalar(pk_hh, m, ba[:, 0:1], None, ALU.add))
            nc.vector.tensor_scalar(bias2, pk_hh, -1.0, ba[:, 0:1], ALU.mult, ALU.add).then_inc(s_peak, 1)

            def att_lo(b):
                dve.wait_ge(s_athi, b + 1)
                nc.vector.tensor_tensor(att_t[:, 1, b], bank[b][:, :], att_t[:, 0, b].bitcast(f32), ALU.subtract
                                        ).then_inc(s_atlo, 1)

            for b in range(NB):
                dve.wait_ge(s_exp, 2 * NB + b + 2)
                step(nc.vector.tensor_tensor(tab_sb[1][:, b], tab_sb[1][:, b], counts[:, 1, b], ALU.mult))
                nc.vector.scalar_tensor_tensor(out=att[:, b], in0=tab_sb[0][:, b], scalar=drop_exp[:, b:b + 1],
                                               in1=tab_sb[1][:, b], op0=ALU.mult, op1=ALU.add,
                                               accum_out=den[:, 0, b:b + 1]).then_inc(s_att, 1)
                if b >= 2:
                    att_lo(b - 2)
            att_lo(NB - 2)
            att_lo(NB - 1)
            dve.wait_ge(s_att, NB)
            step(nc.vector.tensor_scalar(den[:, 0], den[:, 0], TINY, None, ALU.max))
            step(nc.vector.reciprocal(den[:, 1], den[:, 0]))
            dve.wait_ge(s_xre, 32)
            for n in range(NB * NHALF):
                b, half = divmod(n, NHALF)
                cols = slice(half * HALF, (half + 1) * HALF)
                dve.wait_ge(s_fin, n + 1)
                step(nc.vector.scalar_tensor_tensor(out=partial[:, b, cols], in0=bank[(4 + n) % 8][:, :],
                                                    scalar=den[:, 1, b:b + 1], in1=partial[:, b, cols],
                                                    op0=ALU.mult, op1=ALU.add))
                nc.vector.scalar_tensor_tensor(out=partial[:, b, cols], in0=partial[:, b, cols], scalar=0.0,
                                               in1=raw[:, half, b], op0=ALU.max, op1=ALU.add).then_inc(s_out, 1)

        @block.tensor
        def _(pe):
            def products(to, hi, lo, slot, k, first, last):
                nc.tensor.matmul(to, hi, w_hi[:, slot, k], start=first, stop=False)
                nc.tensor.matmul(to, hi, w_lo[:, slot, k], start=False, stop=False)
                return nc.tensor.matmul(to, lo, w_hi[:, slot, k], start=False, stop=last)

            pe.wait_ge(s_iota, 1)
            for b in range(NB):
                pe.wait_ge(s_h, b + 1)
                for k in range(KT):
                    i = nc.tensor.transpose(bank[k][:, b * P:(b + 1) * P], h_sb[:, b, k * P:(k + 1) * P], ident[:, :])
                    if b == NB - 1:
                        i.then_inc(s_tr, 1)
            pe.wait_ge(s_tlo, KT)

            def node_products(base, body, i):
                for j in range(4):
                    pe.wait_ge(s_wlo, base + 4 * i + (j + 1))
                    if j == 0:
                        pe.wait_ge(s_pev, 1 + body + i)
                    if j == 2:
                        pe.wait_ge(s_qev, 1 + body + i)
                    for k in range(KC):
                        kk = KC * (j % 2) + k
                        for b in range(NB):
                            m = products(bank[4 * (j // 2) + b][:, :], h_t[:, 0, kk, b * P:(b + 1) * P],
                                         h_t[:, 1, kk, b * P:(b + 1) * P], j % SPLIT, k, kk == 0, kk == KT - 1)
                    m.then_inc(s_wused, 1)

            with pe.Fori(0, NHALF) as i:
                node_products(PH_HO, 0, i)
            pe.wait_ge(s_hh_rows, 64)
            pe.wait_ge(s_pev, 3)
            pe.wait_ge(s_qev, 3)
            for k in range(KT):
                for j in range(2):
                    side, kk = divmod(2 * k + j, KT)
                    for e in range(T_HH):
                        i = nc.tensor.transpose(bank[k][:, (2 * j + e) * P:(2 * j + e + 1) * P],
                                                hh_rows[:, 2 * side + e, kk * P:(kk + 1) * P], ident[:, :])
                i.then_inc(s_tr, 1)
            pe.wait_ge(s_tlo, 2 * KT)

            def open_counts(banks, start):
                for b in range(NB):
                    i = nc.tensor.matmul(bank[banks + b][:, :], zeros[:, :], node_row[:, :], start=start, stop=not start)
                return i

            def count_group(g, slot, banks):
                pe.wait_ge(s_one, g + 1)
                pe.wait_ge(s_steps, g + 1)
                for j in range(2):
                    for b in range(NB):
                        i = nc.tensor.matmul(bank[banks + b][:, :], rows[:, slot, j, 1, b * P:(b + 1) * P],
                                             rows[:, slot, j, 0], start=False, stop=False)
                i.then_inc(s_oused, 1)

            open_counts(0, True)
            with pe.Fori(0, T_HO // 4) as i:
                for j in range(2):
                    count_group(2 * i + j, j, 0)
            open_counts(0, False).then_inc(s_cnt, 1)
            open_counts(4, True)
            for g in range(T_HO // 2, T_NODE // 2):
                count_group(g, g % 2, 4)
            open_counts(4, False).then_inc(s_cnt, 1)
            pe.wait_ge(s_cev, 1)
            open_counts(0, True)
            count_group(T_NODE // 2, (T_NODE // 2) % 2, 0)
            open_counts(0, False).then_inc(s_cnt, 1)
            pe.wait_ge(s_cev, 3)

            with pe.Fori(0, NHALF) as i:
                node_products(PH_OO, 2, i)
            pe.wait_ge(s_pev, 5)
            pe.wait_ge(s_qev, 5)
            for half in range(NHALF):
                for j in range(4):
                    pe.wait_ge(s_wlo, PH_HH + 4 * half + j + 1)
                    for k in range(KC):
                        kk = KC * j + k
                        for e in range(T_HH):
                            m = products(bank[4 * half + e][:, :], feat_hi[:, kk, e * P:(e + 1) * P],
                                         feat_lo[:, kk, e * P:(e + 1) * P], j % SPLIT, k, kk == 0, kk == 2 * KT - 1)
                    m.then_inc(s_wused, 1)

            for half in range(NHALF):
                pe.wait_ge(s_hhev, half + 1)
                for j in range(4):
                    pe.wait_ge(s_wlo, PH_TOP + 4 * half + j + 1)
                    for k in range(KC):
                        kk = KC * (j // 2) + k
                        for b in (range(0, 1) if j % 2 == 0 else range(1, NB)):
                            m = products(bank[4 * half + b][:, :], h_t[:, 0, kk, b * P:(b + 1) * P],
                                         h_t[:, 1, kk, b * P:(b + 1) * P], j % SPLIT, k, kk == 0, kk == KT - 1)
                    m.then_inc(s_wused, 1)
            for q in range(4):
                if q < 2:
                    pe.wait_ge(s_part, q + 1)
                else:
                    pe.wait_ge(s_gev, q - 1)
                for j in range(2):
                    pe.wait_ge(s_wlo, PH_G + 2 * q + j + 1)
                    for k in range(KC):
                        kk = KC * j + k
                        for b in range(NB):
                            m = products(bank[4 * (q % 2) + b][:, :], h_t[:, 0, kk, b * P:(b + 1) * P],
                                         h_t[:, 1, kk, b * P:(b + 1) * P], j % SPLIT, k, kk == 0, kk == KT - 1)
                    m.then_inc(s_wused, 1)
            pe.wait_ge(s_gev, 3)
            for b in range(NB):
                pe.wait_ge(s_att, b + 1)
                for a in range(NB):
                    i = nc.tensor.transpose(bank[b][:, a * P:(a + 1) * P], att[:, b, a * P:(a + 1) * P], ident[:, :])
                i.then_inc(s_attr, 1)
            pe.wait_ge(s_glo, 2)
            for n in range(NB * NHALF):
                b, half = divmod(n, NHALF)
                kind = 1 if b == 0 else 0
                pe.wait_ge(s_atlo, b + 1 if n < 4 else NB)
                for a in range(NB):
                    hi, lo = att_t[:, 0, b, a * P:(a + 1) * P], att_t[:, 1, b, a * P:(a + 1) * P]
                    to = bank[(4 + n) % 8][:, :]
                    nc.tensor.matmul(to, hi, g_hi[kind][:, half, a], start=a == 0, stop=False)
                    nc.tensor.matmul(to, hi, g_lo[kind][:, half, a], start=False, stop=False)
                    i = nc.tensor.matmul(to, lo, g_hi[kind][:, half, a], start=False, stop=a == NB - 1)
                i.then_inc(s_fin, 1)

        @block.gpsimd
        def _(pool):
            nc.gpsimd.memset(stage[:, 0], EMPTY).then_inc(s_empty, 1)
            nc.gpsimd.memset(ident[:, :], 0.0)
            nc.gpsimd.memset(zeros[:, :], 0.0)
            nc.gpsimd.iota(node_row[:, :], [[1, N]], base=0, channel_multiplier=0,
                           allow_small_or_imprecise_dtypes=True).then_inc(s_now, 1)
            pool.wait_ge(s_now, 1)
            nc.gpsimd.affine_select(out=ident[:, :], in_=ident[:, :], compare_op=ALU.not_equal, fill=1.0, base=0,
                                    pattern=[[-1, P]], channel_multiplier=1).then_inc(s_iota, 1)

            def gather(to, table, nodes, landed):
                nc.gpsimd.indirect_dma_start(to, None, table[:, :], bass.IndirectOffsetOnAxis(ap=nodes, axis=0)
                                             ).then_inc(landed, 16)

            pool.wait_ge(s_index, 1)
            pool.wait_ge(s_hd, 16)
            for side, nodes in ((0, i_src), (1, i_dst)):
                for e in range(T_HH):
                    gather(hh_rows[:, 2 * side + e], h_dram, nodes[:, T_NODE + e:T_NODE + e + 1], s_hh_rows)

            def wait(what, value):
                pool.wait_ge(what, value)
                pool.sem_inc(s_turn, 1)

            def take(t, row, s):
                nc.gpsimd.tensor_copy(index_now[:, s], row).then_inc(s_now, 1)
                wait(s_now, t + 2)

            def gather_tile(kind, s):
                tab_p, tab_q = node_tab[kind]
                gather(edge_p[:, s], tab_p, index_now[:, s, 0:1], s_gath[s])
                gather(edge_q[:, s], tab_q, index_now[:, s, 1:2], s_gath[s])

            def scatter(kind, s):
                nc.gpsimd.indirect_dma_start(pair_tab[kind][:, :], bass.IndirectOffsetOnAxis(ap=index_now[:, s, 2:3], axis=0),
                                             index_now[:, s, 3:4].bitcast(f32), None).then_inc(s_scat, 16)

            pool.wait_ge(s_const, 32)
            pool.wait_ge(s_tabs, 48)
            pool.wait_ge(s_pst, 32)
            pool.wait_ge(s_qst, 32)
            pool.wait_ge(s_tr, 2 * KT)
            def load_table(kind):
                name = ("ho", "oo", "hh")[kind]
                pool.dma_start(tab_sb[kind], pair_tab[name].rearrange("(b p n) o -> p b (n o)", p=P, n=N)
                               ).then_inc(s_tab[kind], 16)

            def next_tile(t, row, s, first=False):
                wait(s_logit, t + (1 - SLOTS))
                take(t, row, s)
                gather_tile("ho", s)
                if not first:
                    wait(s_scat, 16 * t - 16 * SLOTS)
                scatter("ho", s)

            for t in range(SLOTS):
                take(t, index[:, t], t)
                gather_tile("ho", t)
            for t in range(SLOTS, 2 * SLOTS):
                next_tile(t, index[:, t], t % SLOTS, first=t == SLOTS)
            with pool.Fori(2, T_HO // SLOTS) as i:
                for s in range(SLOTS):
                    next_tile(SLOTS * i + s, index[:, bass.ds(SLOTS * i + s, 1)].rearrange("p o c -> p (o c)"), s)
            for t in range(T_HO, T_NODE + SLOTS):
                s = t % SLOTS
                pool.wait_ge(s_logit, t - SLOTS + 1)
                take(t, index[:, t], s)
                if t == T_HO:
                    pool.wait_ge(s_pst, 64)
                    pool.wait_ge(s_qst, 64)
                if t < T_NODE:
                    gather_tile("oo", s)
                pool.wait_ge(s_scat, 16 * (t - SLOTS))
                scatter("ho" if t - SLOTS < T_HO else "oo", s)
                if t == T_HO + SLOTS:
                    pool.wait_ge(s_hhlog, 1)
                    pool.wait_ge(s_scat, 16 * T_HO)
                    load_table(0)
                if t == T_HO + SLOTS + 3:
                    pool.wait_ge(s_hhscat, 16 * T_HH)
                    load_table(2)
                if t == T_HO + SLOTS + 1:
                    pool.wait_ge(s_hhlog, 1)
                    for e in range(T_HH):
                        if e:
                            pool.wait_ge(s_hhscat, 16 * e)
                        nc.gpsimd.indirect_dma_start(pair_tab["hh"][:, :],
                                                     bass.IndirectOffsetOnAxis(ap=pair_hh[:, e:e + 1], axis=0),
                                                     logit_hh[:, e:e + 1], None).then_inc(s_hhscat, 16)
            pool.wait_ge(s_scat, 16 * T_NODE)
            load_table(1)


def kernel(x, src, dst, L0_gnn_W_hh, L0_gnn_b_hh, L0_gnn_W_oo, L0_gnn_b_oo, L0_gnn_W_ho, L0_gnn_b_ho,
           L0_gnn_W_a, L0_gnn_b_a, L0_gnn_W_hn, L0_gnn_b_hn, L0_gnn_W_on, L0_gnn_b_on):
    import numpy as np
    import concourse.bacc as bacc
    from concourse.bass_utils import run_bass_kernel_spmd

    def chunks(w, first, n, half):
        w = np.asarray(w).reshape(2 * KT, P, NHALF, HALF)[first:first + n * KC, :, half]
        return w.reshape(n, KC, P, HALF).transpose(0, 2, 1, 3)

    order = [chunks(w, 0, 4, half) for w in (L0_gnn_W_ho, L0_gnn_W_oo, L0_gnn_W_hh) for half in range(NHALF)]
    order += [chunks(w, k, 1, half) for half in range(NHALF) for k in (0, KC) for w in (L0_gnn_W_hn, L0_gnn_W_on)]
    order += [chunks(w, KT, 2, half) for w in (L0_gnn_W_on, L0_gnn_W_hn) for half in range(NHALF)]
    arrays = {
        "x": np.ascontiguousarray(x), "src": np.ascontiguousarray(src), "dst": np.ascontiguousarray(dst),
        "w_chunks": np.ascontiguousarray(np.concatenate(order)),
        "biases": np.stack([np.asarray(b) for b in (L0_gnn_b_ho, L0_gnn_b_oo, L0_gnn_b_hh, L0_gnn_b_hn, L0_gnn_b_on)]),
        "w_a": np.ascontiguousarray(np.asarray(L0_gnn_W_a).reshape(1, D)),
        "b_a": np.ascontiguousarray(np.asarray(L0_gnn_b_a).reshape(1, 1)),
    }
    nc = bacc.Bacc("TRN2", target_bir_lowering=False, num_devices=1)
    args = [nc.dram_tensor(name, a.shape, mybir.dt.from_np(a.dtype), kind="ExternalInput").ap()
            for name, a in arrays.items()]
    out = nc.dram_tensor("out", (N, D), mybir.dt.float32, kind="ExternalOutput").ap()
    build(nc, *args, out)
    return run_bass_kernel_spmd(nc, [arrays], core_ids=[0]).results[0]["out"]
```

```python
import concourse.bass as bass
from concourse import mybir
from contextlib import ExitStack

P = 128
N, D = 512, 1024
NB = N // P
KT = D // P
HALF = 512
NHALF = D // HALF
E_HH, E_OO = 256, 1280
E_HO = 8704 - E_HH - E_OO
T_HH, T_OO, T_HO = E_HH // P, E_OO // P, E_HO // P
T_ALL = T_HO + T_OO + T_HH
T_NODE = T_HO + T_OO
KC = 4
PH_HO, PH_OO, PH_HH, PH_TOP, PH_G = 0, 8, 16, 24, 32
CHUNKS = 40
RAW = 4
SPLIT = 2
TILES_COUNT = 16
TILES_OO = [4, 2, 2, 3, 2, 3, 2, 2]
TILES_HH = [1] * 8
TILES_TOP = [1] * 8
TILES_G = [3, 2, 2, 2, 2, 3, 0]
PEAK_HH, PEAK_HO = 4, 5
ORDER = (1, 2, 3, 0)
SLOTS = 4
SPLIT_TILES = 16
SPLIT_0 = 32
LATE = 3
EMPTY = -3.0e38
TINY = 1.0e-30
EPS = 1e-5


def build(nc, x, src, dst, w_chunks, biases, w_a, b_a, out):
    f32, f32r, bf16, f16 = mybir.dt.float32, mybir.dt.float32r, mybir.dt.bfloat16, mybir.dt.float16
    i32, i16 = mybir.dt.int32, mybir.dt.int16
    ALU = mybir.AluOpType
    ACT = mybir.ActivationFunctionType
    AX = mybir.AxisListType

    def dram(name, shape):
        return nc.dram_tensor(name, shape, f32, kind="Internal").ap()

    h_dram = dram("h_dram", (N, D))
    node_tab = {"ho": (dram("p_ho", (N, D)), dram("q_ho", (N, D))),
                "oo": (dram("p_oo", (N, D)), dram("q_oo", (N, D)))}
    left_tab = (dram("p_ho_left", (N, HALF)), dram("q_ho_left", (N, HALF)))
    pair_tab = {k: dram(f"pairs_{k}", (N * N, 1)) for k in ("ho", "oo", "hh")}

    with ExitStack() as ctx:
        def sb(name, shape, dt):
            return ctx.enter_context(nc.sbuf_tensor(name, shape, dt))

        def shared(*specs):
            got = []
            for spec in specs[:-1]:
                with nc.sbuf_tensor(*spec) as t:
                    got.append(t)
            return got + [sb(*specs[-1])]

        def sem(name):
            return ctx.enter_context(nc.semaphore(name))

        h_t = sb("h_t", [P, 2, KT, N], f32r)
        g_raw, raw = shared(("g_raw", [P, RAW, KC, HALF], f32r), ("raw", [P, RAW, KC, HALF], f32))
        x_again, w_hi = shared(("x_again", [P, NHALF, NB, HALF], f32), ("w_hi", [P, SPLIT, KC, HALF], f32r))
        w_lo = sb("w_lo", [P, SPLIT, KC, HALF], f32r)
        gath = sb("gath", [P, 2, SLOTS, D], f32)
        feat_hi, partial = shared(("feat_hi", [P, 2 * KT, E_HH], f32r), ("partial", [P, NB, D], f32))
        feat_lo, g_on_left, h_sb = shared(("feat_lo", [P, 2 * KT, E_HH], f32r), ("g_on_left", [P, 2, NB, HALF], f32r),
                                          ("h_sb", [P, NB, D], f32))
        count_buf, att_t, stage = shared(("count_buf", [P, 2, NB, 2, N], bf16), ("att_t", [P, 2, NB, N], f32r),
                                         ("stage", [P, 2, NB, HALF], f32))
        rows = count_buf[:, 0].rearrange("p (g j) s n -> p g j s n", g=2)
        step_sums = count_buf[:, 1].rearrange("p b k n -> p k b n").bitcast(i16)
        counts = sb("counts", [P, 3, NB, N], i16)
        g_on_right, bias = shared(("g_on_right", [P, NB, HALF], f32r), ("bias", [P, 2, D], f32))
        g_split = [(g_on_left[:, 0], g_on_left[:, 1]), (g_on_right[:, :], g_raw[:, 0]), (g_raw[:, 1], g_raw[:, 2]),
                   (h_t[:, 0, 0:NB], h_t[:, 0, NB:2 * NB])]
        att_hi, att_lo = att_t[:, 1], att_t[:, 0]
        wa = sb("wa", [P, D], f32)
        ba = sb("ba", [P, 1], f32)
        ident = sb("ident", [P, P], f32)
        warm = sb("warm", [P, 1], f32)
        zeros = sb("zeros", [P, P], f16)
        node_row = sb("node_row", [P, N], f16)
        i_src = sb("i_src", [P, T_ALL], i32)
        i_dst = sb("i_dst", [P, T_ALL], i32)
        f_src = sb("f_src", [P, T_ALL], f32)
        step_at = sb("step_at", [P, T_ALL], f32)
        f_dst = sb("f_dst", [P, T_ALL], f32)
        index = sb("index", [P, T_NODE + SLOTS, 4], i32)
        left_index = sb("left_index", [P, SPLIT_TILES, 2], i32)
        index_f = index[:, :, :].bitcast(f32)
        pair_hh = sb("pair_hh", [P, T_HH], i32)
        index_now = sb("index_now", [P, SLOTS, 4], i32)
        logit_side = sb("logit_side", [P, NHALF, SPLIT_TILES], f32)
        logit_half = sb("logit_half", [P, NHALF, T_HH], f32)
        logit_hh = sb("logit_hh", [P, T_HH], f32)
        stats = sb("stats", [P, NB, 2, 6], f32)
        mv = sb("mv", [P, NB, 2], f32)
        rstd = sb("rstd", [P, 4, NB], f32)
        peak = sb("peak", [P, 8, NB], f32)
        den = sb("den", [P, 2, NB], f32)

        edge_p, edge_q = gath[:, 0], gath[:, 1]
        x_sb = gath[:, 0]
        hh_rows = gath[:, 1]
        tab_sb = [stage[:, 0], gath[:, 0, 0:2, :].rearrange("p a (b n) -> p (a b) n", n=N), stage[:, 1]]
        att = gath[:, 1, 2:4, :].rearrange("p a (b n) -> p (a b) n", n=N)
        bank = [ctx.enter_context(nc.psum_tensor(f"bank{i}", [P, HALF], f32)) for i in range(8)]

        s_x = [sem(f"x_landed{b}") for b in range(NB)]
        s_idx, s_const, s_bias, s_tabs = sem("indices_landed"), sem("constants_landed"), sem("bias_landed"), sem("pair_tables_cleared")
        s_warm = sem("warm_ready")
        s_empty, s_iota, s_index = sem("empty_ready"), sem("iota_ready"), sem("index_ready")
        s_var, s_std, s_norm, s_h = sem("variance_ready"), sem("std_ready"), sem("norm_ready"), sem("h_ready")
        s_hd, s_hh_rows = sem("h_stored"), sem("hh_rows_landed")
        s_tr, s_thi, s_tlo = sem("transposed"), sem("transposed_hi"), sem("transposed_lo")
        s_raw = [sem(f"raw_landed{i}") for i in range(RAW)]
        s_whi, s_wlo, s_wused = sem("weights_hi"), sem("weights_lo"), sem("weights_used")
        s_pev, s_qev = sem("p_evacuated"), sem("q_evacuated")
        s_pst, s_qst = sem("p_stored"), sem("q_stored")
        s_leftst = [sem("p_left_stored"), sem("q_left_stored")]
        s_steps, s_diff = sem("src_steps_ready"), sem("counts_ready")
        s_one, s_oused, s_cnt, s_cev = sem("onehot_ready"), sem("onehot_used"), sem("counted"), sem("counts_evacuated")
        s_gath = [sem(f"edge_rows_landed{i}") for i in range(SLOTS)]
        s_now, s_esum, s_logit, s_scat = sem("index_now_ready"), sem("edge_summed"), sem("logit_ready"), sem("logits_scattered")
        s_half = [sem(f"half_rows_landed{i}") for i in range(SLOTS)]
        s_halfnow, s_halfsum, s_left, s_right = sem("half_index_ready"), sem("half_summed"), sem("left_logit_ready"), sem("right_logit_ready")
        s_hhlog, s_hhscat = sem("hh_logits_ready"), sem("hh_scattered")
        s_hhev, s_hhhalf = sem("hh_evacuated"), sem("hh_half_logits")
        s_weighed, s_esums = sem("early_exps_weighed"), sem("early_exps_summed")
        s_part = sem("partial_ready")
        s_xre, s_ghi, s_glo = sem("x_reloaded"), sem("g_hi_ready"), sem("g_lo_ready")
        s_tab = [sem(f"table_loaded_{kind}") for kind in pair_tab]
        s_peak, s_exp, s_att, s_attr = sem("peak_ready"), sem("exp_ready"), sem("att_ready"), sem("att_transposed")
        s_athi, s_atlo = sem("att_hi"), sem("att_lo")
        s_fin, s_out, s_stored = sem("product_ready"), sem("out_ready"), sem("out_stored")
        s_dve, s_turn = sem("vector_step"), sem("pool_turns")

        block = ctx.enter_context(nc.Block())

        def blocks(t):
            return t.rearrange("(b p) d -> p b d", p=P)

        @block.sync
        def _(sp):
            for b in range(NB):
                sp.dma_start(x_sb[:, b], x[b * P:(b + 1) * P, :]).then_inc(s_x[b], 16)
            for c in range(2):
                sp.dma_start(raw[:, c], w_chunks[c]).then_inc(s_raw[c], 16)
            for t0, tiles, e0 in ((0, T_HO, E_HH + E_OO), (T_HO, T_OO, E_HH), (T_NODE, T_HH, 0)):
                for to, of in ((i_src, src), (i_dst, dst)):
                    sp.dma_start(to[:, t0:t0 + tiles], of[e0:e0 + tiles * P].rearrange("(p t) -> p t", p=P)
                                  ).then_inc(s_idx, 16)
            for c in range(2, RAW):
                sp.dma_start(raw[:, c], w_chunks[c]).then_inc(s_raw[c], 16)
            sp.dma_start(wa[:, :], w_a.to_broadcast((P, D))).then_inc(s_const, 16)
            sp.dma_start(ba[:, :], b_a.to_broadcast((P, 1))).then_inc(s_const, 16)
            for n in range(2):
                sp.dma_start(bias[:, n], biases[n:n + 1, :].to_broadcast((P, D))).then_inc(s_bias, 16)
            sp.wait_ge(s_h, NB)
            sp.dma_start(blocks(h_dram), h_sb[:, :, :]).then_inc(s_hd, 16)
            sp.wait_ge(s_empty, 1)
            for t in pair_tab.values():
                sp.dma_start(t.rearrange("(p n) o -> p (n o)", p=P), stage[:, 0].rearrange("p b n -> p (b n)")
                              ).then_inc(s_tabs, 16)
            with sp.Fori(1, CHUNKS // RAW) as i:
                for s in range(RAW):
                    sp.wait_ge(s_wlo, 2 * RAW * i + 2 * (s + 1 - RAW))
                    sp.dma_start(raw[:, s], w_chunks[bass.ds(RAW * i + s, 1)].rearrange("o p k n -> (o p) k n")
                                 ).then_inc(s_raw[s], 16)
            for n in range(NB * NHALF):
                b, half = ORDER[n // NHALF], n % NHALF
                sp.wait_ge(s_out, n + 1)
                sp.dma_start(out[b * P:(b + 1) * P, half * HALF:(half + 1) * HALF],
                             partial[:, b, half * HALF:(half + 1) * HALF]).then_inc(s_stored, 16)
            sp.wait_ge(s_stored, 16 * NB * NHALF)

        @block.scalar
        def _(act):
            act.wait_ge(s_warm, 1)
            nc.scalar.activation(warm[:, :], warm[:, :], ACT.Sqrt)

            def std(b):
                act.wait_ge(s_var, b + 1)
                nc.scalar.activation(rstd[:, 1, b:b + 1], rstd[:, 0, b:b + 1], ACT.Sqrt).then_inc(s_std, 1)

            for b in range(NB):
                if b % 2 == 0:
                    std(b)
                    std(b + 1)
                act.wait_ge(s_norm, b // 2 + 1)
                nc.scalar.activation(h_sb[:, b], x_sb[:, b], ACT.Relu, bias=rstd[:, 3, b:b + 1],
                                     scale=rstd[:, 2, b:b + 1]).then_inc(s_h, 1)

            def split_hi(c, parts=(0, 1)):
                act.wait_ge(s_raw[c % RAW], 16 * (c // RAW + 1))
                if c >= SPLIT:
                    act.wait_ge(s_wused, c - SPLIT + 1)
                for n in parts:
                    k = slice(n * KC // 2, (n + 1) * KC // 2)
                    nc.scalar.activation(w_hi[:, c % SPLIT, k], raw[:, c % RAW, k], ACT.Copy).then_inc(s_whi, 1)

            def transposed_hi(first):
                for k in range(first, first + KT // 2):
                    act.wait_ge(s_tr, k + 1)
                    nc.scalar.activation(h_t[:, 0, k], bank[k][:, :], ACT.Copy).then_inc(s_thi, 1)

            split_hi(0, (0,))
            transposed_hi(0)
            split_hi(0, (1,))
            transposed_hi(KT // 2)
            act.sem_inc(s_qev, 1)

            def store_half(tab, half, side):
                act.dma_start(blocks(tab)[:, :, half * HALF:(half + 1) * HALF], stage[:, side]
                              ).then_inc((s_pst, s_qst)[side], 16)

            def store_left(side):
                act.dma_start(blocks(left_tab[side]), stage[:, side]).then_inc(s_leftst[side], 16)

            def store_p(n, kind):
                act.wait_ge(s_pev, n + 2)
                if n == 0:
                    store_left(0)
                store_half(node_tab[kind][0], n % 2, 0)

            def evacuate_q(n, kind):
                act.wait_ge(s_wused, 4 * (n + 1))
                if n:
                    act.wait_ge(s_qst, 16 * n)
                    act.wait_ge(s_leftst[1], 16)
                else:
                    act.wait_ge(s_tabs, 48)
                for b in range(NB):
                    i = nc.scalar.activation(stage[:, 1, b], bank[4 + b][:, :], ACT.Copy)
                i.then_inc(s_qev, 1)
                act.wait_ge(s_qev, n + 2)
                if n == 0:
                    store_left(1)
                store_half(node_tab[kind][1], n % 2, 1)

            for c in range(1, 4):
                split_hi(c)
            store_p(0, "ho")
            split_hi(4)
            evacuate_q(0, "ho")
            split_hi(5)
            split_hi(6)
            split_hi(7)
            store_p(1, "ho")
            act.dma_start(bias[:, 0], biases[2:3, :].to_broadcast((P, D))).then_inc(s_bias, 16)
            split_hi(8)

            def src_steps(g, slot, used):
                if used is not None:
                    act.wait_ge(s_oused, used)
                for j in range(2):
                    i = nc.scalar.activation(rows[:, slot, j, 0], node_row[:, :], ACT.Sign,
                                             bias=step_at[:, bass.ds(2 * g + j, 1)])
                i.then_inc(s_steps, 1)

            def evacuate_sums(kind, banks, slot):
                act.wait_ge(s_cnt, kind + 1)
                if kind >= 2:
                    act.wait_ge(s_diff, kind - 1)
                for b in range(NB):
                    i = nc.scalar.activation(step_sums[:, slot, b], bank[banks + b][:, :], ACT.Copy)
                i.then_inc(s_cev, 1)

            def feature_hi(first):
                for k in range(first, first + KT // 2):
                    act.wait_ge(s_tr, KT + k + 1)
                    nc.scalar.activation(feat_hi[:, 2 * k:2 * k + 2].rearrange("p k e -> p (k e)"), bank[k % 4][:, :],
                                         ACT.Copy).then_inc(s_thi, 1)

            act.wait_ge(s_index, 1)
            act.wait_ge(s_iota, 1)
            act.wait_ge(s_pst, 32)
            src_steps(0, 0, None)
            src_steps(1, 1, None)
            evacuate_q(1, "ho")
            feature_hi(0)
            src_steps(2, 0, 1)
            src_steps(3, 1, 2)
            feature_hi(KT // 2)
            with act.Fori(2, T_HO // 4) as i:
                for j in range(2):
                    src_steps(2 * i + j, j, 2 * i + (j - 1))
            for g in range(T_HO // 2, T_ALL // 2):
                src_steps(g, g % 2, g - 1)
            act.wait_ge(s_qst, 32)
            evacuate_sums(0, 4, 0)
            evacuate_sums(1, 0, 1)
            evacuate_sums(2, 4, 0)
            split_hi(9)
            for n in (2, 3):
                split_hi(4 * n + 2)
                split_hi(4 * n + 3)
                store_p(n, "oo")
                split_hi(4 * n + 4)
                evacuate_q(n, "oo")
                split_hi(4 * n + 5)
            for c in range(18, 28):
                split_hi(c)
            act.wait_ge(s_hhlog, 1)
            for n in range(2):
                act.dma_start(bias[:, n], biases[3 + n:4 + n, :].to_broadcast((P, D))).then_inc(s_bias, 16)
            for c in range(28, 36):
                split_hi(c)

            def g_hi(q):
                act.wait_ge(s_wused, PH_G + 2 * q + 2)
                if q == 1:
                    act.wait_ge(s_part, 2)
                if q == 2:
                    act.wait_ge(s_wlo, 2 * (CHUNKS - 2))
                for b in range(NB):
                    i = nc.scalar.activation(g_split[q][0][:, b], bank[4 * (q % 2) + b][:, :], ACT.Copy)
                i.then_inc(s_ghi, 1)

            def exps(kind, ready, bias_at, order=range(NB)):
                act.wait_ge(s_peak, ready)
                for b in order:
                    nc.scalar.activation(tab_sb[kind][:, b], tab_sb[kind][:, b], ACT.Exp,
                                         bias=peak[:, bias_at, b:b + 1]).then_inc(s_exp, 1)

            g_hi(0)
            split_hi(36)
            split_hi(37)
            g_hi(1)
            split_hi(38)
            split_hi(39)
            g_hi(2)

            exps(0, 1, 4)
            exps(2, 1, 4)
            g_hi(3)
            act.wait_ge(s_peak, 2)
            nc.scalar.activation(peak[:, 7], peak[:, 6], ACT.Exp).then_inc(s_exp, 1)
            exps(1, 2, 5, ORDER)
            act.wait_ge(s_wused, CHUNKS)
            for half in range(NHALF):
                act.dma_start(x_again[:, half], blocks(x)[:, :, half * HALF:(half + 1) * HALF]).then_inc(s_xre, 16)
            for n, b in enumerate(ORDER):
                act.wait_ge(s_attr, n + 1)
                nc.scalar.activation(att_hi[:, b], bank[b][:, :], ACT.Copy).then_inc(s_athi, 1)

        @block.vector
        def _(dve):
            steps = [0]

            def step(i):
                steps[0] += 1
                i.then_inc(s_dve, 1)
                dve.wait_ge(s_dve, steps[0])

            def variance(b):
                dve.wait_ge(s_x[b], 16)
                for j in range(2):
                    i = nc.vector.bn_stats(stats[:, b, j], x_sb[:, b, j * HALF:(j + 1) * HALF])
                step(i)
                step(nc.vector.bn_aggr(mv[:, b], stats[:, b]))
                nc.vector.tensor_scalar(rstd[:, 0, b:b + 1], mv[:, b, 1:2], EPS, None, ALU.add).then_inc(s_var, 1)

            for b in range(0, NB, 2):
                pair = slice(b, b + 2)
                variance(b)
                variance(b + 1)
                dve.wait_ge(s_std, b + 2)
                var, half, r = (rstd[:, n, pair] for n in range(3))
                step(nc.vector.reciprocal(r, half))
                step(nc.vector.tensor_tensor(half, r, r, ALU.mult))
                step(nc.vector.tensor_tensor(half, half, var, ALU.mult))
                step(nc.vector.tensor_scalar(half, half, -0.5, 1.5, ALU.mult, ALU.add))
                step(nc.vector.tensor_tensor(r, r, half, ALU.mult))
                nc.vector.scalar_tensor_tensor(out=rstd[:, 3, pair], in0=mv[:, pair, 0], scalar=-1.0, in1=r,
                                               op0=ALU.mult, op1=ALU.mult).then_inc(s_norm, 1)
            def split_lo(c, parts=(0, 1)):
                for n in parts:
                    k = slice(n * KC // 2, (n + 1) * KC // 2)
                    dve.wait_ge(s_whi, 2 * c + (n + 1))
                    nc.vector.tensor_tensor(w_lo[:, c % SPLIT, k], raw[:, c % RAW, k],
                                            w_hi[:, c % SPLIT, k].bitcast(f32), ALU.subtract).then_inc(s_wlo, 1)

            def transposed_lo(first):
                for k in range(first, first + KT // 2):
                    dve.wait_ge(s_thi, k + 1)
                    nc.vector.tensor_tensor(h_t[:, 1, k], bank[k][:, :], h_t[:, 0, k].bitcast(f32), ALU.subtract
                                            ).then_inc(s_tlo, 1)

            split_lo(0, (0,))
            transposed_lo(0)
            dve.sem_inc(s_pev, 1)
            split_lo(0, (1,))
            transposed_lo(KT // 2)
            split_lo(1)
            dve.wait_ge(s_idx, 16 * 6)
            step(nc.vector.memset(index[:, :, :], 0))
            nc.vector.tensor_copy(f_src[:, :], i_src[:, :])
            nc.vector.tensor_copy(f_dst[:, :], i_dst[:, :])
            nc.vector.tensor_copy(index[:, 0:T_NODE, 0], i_src[:, 0:T_NODE])
            step(nc.vector.tensor_copy(index[:, 0:T_NODE, 1], i_dst[:, 0:T_NODE]))
            for side, nodes in enumerate((f_src, f_dst)):
                nc.vector.tensor_copy(left_index[:, :, side], nodes[:, SPLIT_0:SPLIT_0 + SPLIT_TILES])
                nc.vector.tensor_scalar(index[:, SPLIT_0:SPLIT_0 + SPLIT_TILES, side],
                                        nodes[:, SPLIT_0:SPLIT_0 + SPLIT_TILES], 2.0, 1.0, ALU.mult, ALU.add)
            nc.vector.tensor_scalar(step_at[:, :], f_src[:, :], -1.0, 0.5, ALU.mult, ALU.add)
            nc.vector.scalar_tensor_tensor(out=index[:, SLOTS:SLOTS + T_NODE, 2], in0=f_dst[:, 0:T_NODE],
                                           scalar=float(N), in1=f_src[:, 0:T_NODE], op0=ALU.mult, op1=ALU.add)
            nc.vector.scalar_tensor_tensor(out=pair_hh[:, :], in0=f_dst[:, T_NODE:T_ALL], scalar=float(N),
                                           in1=f_src[:, T_NODE:T_ALL], op0=ALU.mult, op1=ALU.add).then_inc(s_index, 1)

            def evacuate_p(n, half, slot):
                dve.wait_ge(s_wused, 4 * n + 2)
                for b in range(NB):
                    i = nc.vector.tensor_tensor(stage[:, 0, b], bank[b][:, :], bias[:, slot, bass.ds(half * HALF, HALF)],
                                                ALU.add)
                i.then_inc(s_pev, 1)

            def edge_logit(p, q, t):
                dve.wait_ge(s_esum, t + 1)
                nc.vector.scalar_tensor_tensor(out=q, in0=p, scalar=0.0, in1=wa[:, :], op0=ALU.max, op1=ALU.mult,
                                               accum_out=index_f[:, bass.ds(t + SLOTS, 1), 3]).then_inc(s_logit, 1)

            def edges(n, t, s, landed):
                for j in range(n):
                    slot = (s + j) % SLOTS
                    dve.wait_ge(s_gath[slot], landed + 32 * ((s + j) // SLOTS))
                    p, q = edge_p[:, slot], edge_q[:, slot]
                    nc.vector.tensor_tensor(p, p, q, ALU.add).then_inc(s_esum, 1)
                    edge_logit(p, q, t + j)

            def half_edges(n, t):
                for t in range(t, t + n):
                    slot = t % SLOTS
                    dve.wait_ge(s_half[slot], 32 * (t // SLOTS) + 32)
                    p, q = edge_p[:, slot, 0:HALF], edge_p[:, slot, HALF:D]
                    nc.vector.tensor_tensor(p, p, q, ALU.add).then_inc(s_halfsum, 1)
                    dve.wait_ge(s_halfsum, t + 1)
                    nc.vector.scalar_tensor_tensor(out=q, in0=p, scalar=0.0, in1=wa[:, 0:HALF], op0=ALU.max, op1=ALU.mult,
                                                   accum_out=logit_side[:, 0, t:t + 1]).then_inc(s_left, 1)

            def right_edges(t):
                slot, landed, n = t % SLOTS, 32 * (t // SLOTS) + 32, t - SPLIT_0
                dve.wait_ge(s_gath[slot], landed)
                p, q = edge_p[:, slot, HALF:D], edge_q[:, slot, HALF:D]
                nc.vector.tensor_tensor(p, p, q, ALU.add).then_inc(s_esum, 1)
                dve.wait_ge(s_esum, t + 1)
                nc.vector.scalar_tensor_tensor(out=q, in0=p, scalar=0.0, in1=wa[:, HALF:D], op0=ALU.max, op1=ALU.mult,
                                               accum_out=logit_side[:, 1, n:n + 1]).then_inc(s_right, 1)
                dve.wait_ge(s_right, n + 1)
                nc.vector.tensor_tensor(index_f[:, t + SLOTS, 3:4], logit_side[:, 0, n:n + 1],
                                        logit_side[:, 1, n:n + 1], ALU.add).then_inc(s_logit, 1)

            split_lo(2)
            split_lo(3)
            dve.wait_ge(s_bias, 32)
            dve.wait_ge(s_tabs, 48)
            evacuate_p(0, 0, 0)
            for c in range(4, 7):
                split_lo(c)
            dve.wait_ge(s_const, 32)
            half_edges(3, 0)
            split_lo(7)
            dve.wait_ge(s_pst, 16)
            dve.wait_ge(s_leftst[0], 16)
            evacuate_p(1, 1, 0)
            half_edges(5, 3)
            split_lo(8)
            dve.wait_ge(s_iota, 1)
            dve.wait_ge(s_pst, 32)

            def feature_lo(first):
                for k in range(first, first + KT // 2):
                    dve.wait_ge(s_thi, KT + k + 1)
                    hi, lo = (t[:, 2 * k:2 * k + 2].rearrange("p k e -> p (k e)") for t in (feat_hi, feat_lo))
                    nc.vector.tensor_tensor(lo, bank[k % 4][:, :], hi.bitcast(f32), ALU.subtract).then_inc(s_tlo, 1)

            def one_hot(g, slot, used):
                if used is not None:
                    dve.wait_ge(s_oused, used)
                for j in range(2):
                    i = nc.vector.tensor_scalar(rows[:, slot, j, 1], node_row[:, :],
                                                f_dst[:, bass.ds(2 * g + j, 1)], None, ALU.is_equal)
                i.then_inc(s_one, 1)

            one_hot(0, 0, None)
            one_hot(1, 1, None)
            half_edges(SPLIT_TILES - 8 - LATE, 8)
            def difference(n, kind, slot):
                dve.wait_ge(s_cev, n)
                sums = step_sums[:, slot]
                nc.vector.tensor_tensor(counts[:, kind, :, 1:N], sums[:, :, 1:N], sums[:, :, 0:N - 1], ALU.subtract)
                nc.vector.tensor_tensor(counts[:, kind, :, 0:1], sums[:, :, 0:1], sums[:, :, N - 1:N], ALU.add
                                        ).then_inc(s_diff, 1)

            feature_lo(0)
            one_hot(2, 0, 1)
            one_hot(3, 1, 2)
            half_edges(LATE, SPLIT_TILES - LATE)
            feature_lo(KT // 2)
            with dve.Fori(0, 3) as i:
                for s in range(SLOTS):
                    for j in range(2):
                        one_hot(8 * i + 2 * s + j + 4, j, 8 * i + 2 * s + j + 3)
                    edges(1, 4 * i + s, s, 32 * i + 32)
            for s in range(SLOTS):
                for g in range(28 + 2 * s, min(30 + 2 * s, T_ALL // 2)):
                    one_hot(g, g % 2, g - 1)
                edges(1, 12 + s, s, 32 * 3 + 32)
            for n, kind in enumerate((0, 1, 2)):
                difference(n + 1, kind, n % 2)
            done = [TILES_COUNT]

            def tiles(n):
                for t in range(done[0], done[0] + n):
                    if SPLIT_0 <= t < SPLIT_0 + SPLIT_TILES:
                        right_edges(t)
                    else:
                        edges(1, t, t % SLOTS, 32 * (t // SLOTS) + 32)
                done[0] += n

            split_lo(9)
            for j in range(8):
                tiles(TILES_OO[j])
                split_lo(10 + j)
                if j in (1, 5):
                    half = j // 4
                    dve.wait_ge(s_pst, 32 + 16 * half)
                    dve.wait_ge(s_oused, 34)
                    evacuate_p(2 + half, half, 1)
            for half in range(NHALF):
                for j in range(4):
                    c = 18 + 4 * half + j
                    tiles(TILES_HH[4 * half + j])
                    split_lo(c)
                    if j == 3:
                        dve.wait_ge(s_bias, 48)
                        dve.wait_ge(s_pst, 64)
                        dve.wait_ge(s_qst, 64)
                        dve.wait_ge(s_wused, PH_HH + 4 * half + 4)
                        for e in range(T_HH):
                            i = nc.vector.tensor_tensor(stage[:, 0, e], bank[4 * half + e][:, :],
                                                        bias[:, 0, half * HALF:(half + 1) * HALF], ALU.add)
                        i.then_inc(s_hhev, 1)
                        dve.wait_ge(s_hhev, half + 1)
                        for e in range(T_HH):
                            i = nc.vector.scalar_tensor_tensor(out=stage[:, 1, e], in0=stage[:, 0, e], scalar=0.0,
                                                               in1=wa[:, half * HALF:(half + 1) * HALF],
                                                               op0=ALU.max, op1=ALU.mult,
                                                               accum_out=logit_half[:, half, e:e + 1])
                        i.then_inc(s_hhhalf, 1)
                        dve.wait_ge(s_hhhalf, half + 1)
            nc.vector.tensor_tensor(logit_hh[:, :], logit_half[:, 0], logit_half[:, 1], ALU.add).then_inc(s_hhlog, 1)
            for j in range(8):
                tiles(TILES_TOP[j])
                split_lo(26 + j)
                if j in (3, 7):
                    half = j // 4
                    dve.wait_ge(s_bias, 80)
                    dve.wait_ge(s_wused, PH_TOP + 4 * half + 4)
                    for b in range(NB):
                        i = nc.vector.tensor_tensor(partial[:, b, half * HALF:(half + 1) * HALF], bank[4 * half + b][:, :],
                                                    bias[:, min(b, 1), half * HALF:(half + 1) * HALF], ALU.add)
                    i.then_inc(s_part, 1)
            def g_lo(q):
                dve.wait_ge(s_ghi, q + 1)
                for b in range(NB):
                    i = nc.vector.tensor_tensor(g_split[q][1][:, b], bank[4 * (q % 2) + b][:, :],
                                                g_split[q][0][:, b].bitcast(f32), ALU.subtract)
                i.then_inc(s_glo, 1)

            pk_ho, pk_hh, m1, m, bias1, bias2, drop, drop_exp = (peak[:, n] for n in range(8))

            def early_peak(kind, to):
                dve.wait_ge(s_tab[kind], 16)
                return nc.vector.tensor_reduce(to, tab_sb[kind], AX.X, ALU.max)

            for j in range(7):
                tiles(TILES_G[j])
                if j < 6:
                    split_lo(34 + j)
                if j in (1, 3, 5):
                    g_lo(j // 2)
                if j == PEAK_HH:
                    early_peak(2, pk_hh)
                if j == PEAK_HO:
                    step(early_peak(0, pk_ho))
                    step(nc.vector.tensor_tensor(m1, pk_ho, pk_hh, ALU.max))
                    step(nc.vector.tensor_scalar(m, m1, ba[:, 0:1], None, ALU.add))
                    nc.vector.tensor_scalar(bias1, m, -1.0, ba[:, 0:1], ALU.mult, ALU.add).then_inc(s_peak, 1)
            for n, kind in enumerate((0, 2)):
                for b in range(NB):
                    dve.wait_ge(s_exp, NB * n + b + 1)
                    i = nc.vector.tensor_tensor(tab_sb[kind][:, b], tab_sb[kind][:, b], counts[:, kind, b], ALU.mult)
            i.then_inc(s_weighed, 1)
            tiles(T_NODE - done[0])
            dve.wait_ge(s_tab[1], 16)
            step(nc.vector.tensor_reduce(pk_ho, tab_sb[1], AX.X, ALU.max))
            step(nc.vector.tensor_tensor(m, m1, pk_ho, ALU.max))
            nc.vector.tensor_tensor(drop, m1, m, ALU.subtract)
            step(nc.vector.tensor_scalar(pk_hh, m, ba[:, 0:1], None, ALU.add))
            nc.vector.tensor_scalar(bias2, pk_hh, -1.0, ba[:, 0:1], ALU.mult, ALU.add).then_inc(s_peak, 1)

            g_lo(3)

            def lower_att(n):
                b = ORDER[n]
                dve.wait_ge(s_athi, n + 1)
                nc.vector.tensor_tensor(att_lo[:, b], bank[b][:, :], att_hi[:, b].bitcast(f32), ALU.subtract
                                        ).then_inc(s_atlo, 1)

            for n, b in enumerate(ORDER):
                dve.wait_ge(s_exp, 2 * NB + n + 2)
                step(nc.vector.tensor_tensor(tab_sb[1][:, b], tab_sb[1][:, b], counts[:, 1, b], ALU.mult))
                dve.wait_ge(s_esums, n + 1)
                nc.vector.scalar_tensor_tensor(out=att[:, b], in0=tab_sb[0][:, b], scalar=drop_exp[:, b:b + 1],
                                               in1=tab_sb[1][:, b], op0=ALU.mult, op1=ALU.add,
                                               accum_out=den[:, 0, b:b + 1]).then_inc(s_att, 1)
                if n:
                    lower_att(n - 1)
            lower_att(NB - 1)
            dve.wait_ge(s_att, NB)
            step(nc.vector.tensor_scalar(den[:, 0], den[:, 0], TINY, None, ALU.max))
            step(nc.vector.reciprocal(den[:, 1], den[:, 0]))
            dve.wait_ge(s_xre, 32)
            for n in range(NB * NHALF):
                b, half = ORDER[n // NHALF], n % NHALF
                cols = slice(half * HALF, (half + 1) * HALF)
                dve.wait_ge(s_fin, n + 1)
                step(nc.vector.scalar_tensor_tensor(out=partial[:, b, cols], in0=bank[(4 + n) % 8][:, :],
                                                    scalar=den[:, 1, b:b + 1], in1=partial[:, b, cols],
                                                    op0=ALU.mult, op1=ALU.add))
                nc.vector.scalar_tensor_tensor(out=partial[:, b, cols], in0=partial[:, b, cols], scalar=0.0,
                                               in1=x_again[:, half, b], op0=ALU.max, op1=ALU.add).then_inc(s_out, 1)

        @block.tensor
        def _(pe):
            def products(to, hi, lo, slot, k, first, last):
                nc.tensor.matmul(to, hi, w_hi[:, slot, k], start=first, stop=False)
                nc.tensor.matmul(to, hi, w_lo[:, slot, k], start=False, stop=False)
                return nc.tensor.matmul(to, lo, w_hi[:, slot, k], start=False, stop=last)

            pe.wait_ge(s_iota, 1)
            for b in range(NB):
                pe.wait_ge(s_h, b + 1)
                for k in range(KT):
                    i = nc.tensor.transpose(bank[k][:, b * P:(b + 1) * P], h_sb[:, b, k * P:(k + 1) * P], ident[:, :])
                    if b == NB - 1:
                        i.then_inc(s_tr, 1)

            def weights(chunk, k):
                if k % (KC // 2) == 0:
                    pe.wait_ge(s_wlo, 2 * chunk + (k // (KC // 2) + 1))

            def node_products(base, body, i):
                for j in range(4):
                    if j == 0:
                        pe.wait_ge(s_pev, 1 + body + i)
                    if j == 2:
                        pe.wait_ge(s_qev, 1 + body + i)
                        if base == PH_OO:
                            pe.wait_ge(s_cev, 3)
                    for k in range(KC):
                        kk = KC * (j % 2) + k
                        weights(base + 4 * i + j, k)
                        if j < 2 and base == PH_HO:
                            pe.wait_ge(s_tlo, max(kk + 1, KT // 2))
                        for b in range(NB):
                            m = products(bank[4 * (j // 2) + b][:, :], h_t[:, 0, kk, b * P:(b + 1) * P],
                                         h_t[:, 1, kk, b * P:(b + 1) * P], j % SPLIT, k, kk == 0, kk == KT - 1)
                    m.then_inc(s_wused, 1)

            with pe.Fori(0, NHALF) as i:
                node_products(PH_HO, 0, i)
            def open_counts(banks, start):
                for b in range(NB):
                    i = nc.tensor.matmul(bank[banks + b][:, :], zeros[:, :], node_row[:, :], start=start, stop=not start)
                return i

            def count_group(g, slot, banks):
                pe.wait_ge(s_one, g + 1)
                pe.wait_ge(s_steps, g + 1)
                for j in range(2):
                    for b in range(NB):
                        i = nc.tensor.matmul(bank[banks + b][:, :], rows[:, slot, j, 1, b * P:(b + 1) * P],
                                             rows[:, slot, j, 0], start=False, stop=False)
                i.then_inc(s_oused, 1)

            def transpose_rows(first):
                for k in range(first, first + KT // 2):
                    for j in range(2):
                        side, kk = divmod(2 * k + j, KT)
                        for e in range(T_HH):
                            i = nc.tensor.transpose(bank[k % 4][:, (2 * j + e) * P:(2 * j + e + 1) * P],
                                                    hh_rows[:, 2 * side + e, kk * P:(kk + 1) * P], ident[:, :])
                    i.then_inc(s_tr, 1)

            pe.wait_ge(s_pev, 3)
            pe.wait_ge(s_hh_rows, 64)
            transpose_rows(0)
            pe.wait_ge(s_qev, 3)
            open_counts(4, True)
            count_group(0, 0, 4)
            count_group(1, 1, 4)
            pe.wait_ge(s_tlo, KT + KT // 2)
            transpose_rows(KT // 2)
            count_group(2, 0, 4)
            count_group(3, 1, 4)
            with pe.Fori(2, T_HO // 4) as i:
                for j in range(2):
                    count_group(2 * i + j, j, 4)
            open_counts(4, False).then_inc(s_cnt, 1)
            pe.wait_ge(s_tlo, 2 * KT)
            open_counts(0, True)
            for g in range(T_HO // 2, T_NODE // 2):
                count_group(g, g % 2, 0)
            open_counts(0, False).then_inc(s_cnt, 1)
            pe.wait_ge(s_cev, 1)
            open_counts(4, True)
            count_group(T_NODE // 2, (T_NODE // 2) % 2, 4)
            open_counts(4, False).then_inc(s_cnt, 1)
            pe.wait_ge(s_cev, 2)

            with pe.Fori(0, NHALF) as i:
                node_products(PH_OO, 2, i)
            pe.wait_ge(s_pev, 5)
            pe.wait_ge(s_qev, 5)
            for half in range(NHALF):
                for j in range(4):
                    for k in range(KC):
                        weights(PH_HH + 4 * half + j, k)
                        kk = KC * j + k
                        for e in range(T_HH):
                            m = products(bank[4 * half + e][:, :], feat_hi[:, kk, e * P:(e + 1) * P],
                                         feat_lo[:, kk, e * P:(e + 1) * P], j % SPLIT, k, kk == 0, kk == 2 * KT - 1)
                    m.then_inc(s_wused, 1)

            for half in range(NHALF):
                pe.wait_ge(s_hhev, half + 1)
                for j in range(4):
                    for k in range(KC):
                        weights(PH_TOP + 4 * half + j, k)
                        kk = KC * (j // 2) + k
                        for b in (range(0, 1) if j % 2 == 0 else range(1, NB)):
                            m = products(bank[4 * half + b][:, :], h_t[:, 0, kk, b * P:(b + 1) * P],
                                         h_t[:, 1, kk, b * P:(b + 1) * P], j % SPLIT, k, kk == 0, kk == KT - 1)
                    m.then_inc(s_wused, 1)
            for q in range(4):
                if q < 2:
                    pe.wait_ge(s_part, q + 1)
                else:
                    pe.wait_ge(s_glo, q - 1)
                for j in range(2):
                    for k in range(KC):
                        weights(PH_G + 2 * q + j, k)
                        kk = KC * j + k
                        for b in range(NB):
                            m = products(bank[4 * (q % 2) + b][:, :], h_t[:, 0, kk, b * P:(b + 1) * P],
                                         h_t[:, 1, kk, b * P:(b + 1) * P], j % SPLIT, k, kk == 0, kk == KT - 1)
                    m.then_inc(s_wused, 1)
            pe.wait_ge(s_glo, 3)
            for n, b in enumerate(ORDER):
                pe.wait_ge(s_att, n + 1)
                for a in range(NB):
                    i = nc.tensor.transpose(bank[b][:, a * P:(a + 1) * P], att[:, b, a * P:(a + 1) * P], ident[:, :])
                i.then_inc(s_attr, 1)
            pe.wait_ge(s_glo, 4)
            for n in range(NB * NHALF):
                b, half = ORDER[n // NHALF], n % NHALF
                g_parts = g_split[half if b else 2 + half]
                pe.wait_ge(s_atlo, n // NHALF + 1 if n < 4 else NB)
                for a in range(NB):
                    hi, lo = att_hi[:, b, a * P:(a + 1) * P], att_lo[:, b, a * P:(a + 1) * P]
                    to = bank[(4 + n) % 8][:, :]
                    nc.tensor.matmul(to, hi, g_parts[0][:, a], start=a == 0, stop=False)
                    nc.tensor.matmul(to, hi, g_parts[1][:, a], start=False, stop=False)
                    i = nc.tensor.matmul(to, lo, g_parts[0][:, a], start=False, stop=a == NB - 1)
                i.then_inc(s_fin, 1)

        @block.gpsimd
        def _(pool):
            nc.gpsimd.memset(warm[:, :], 1.0).then_inc(s_warm, 1)
            nc.gpsimd.memset(stage[:, 0], EMPTY).then_inc(s_empty, 1)
            nc.gpsimd.memset(ident[:, :], 0.0)
            nc.gpsimd.memset(zeros[:, :], 0.0)
            nc.gpsimd.iota(node_row[:, :], [[1, N]], base=0, channel_multiplier=0,
                           allow_small_or_imprecise_dtypes=True).then_inc(s_now, 1)
            pool.wait_ge(s_now, 1)
            nc.gpsimd.affine_select(out=ident[:, :], in_=ident[:, :], compare_op=ALU.not_equal, fill=1.0, base=0,
                                    pattern=[[-1, P]], channel_multiplier=1).then_inc(s_iota, 1)

            def gather(to, table, nodes, landed):
                nc.gpsimd.indirect_dma_start(to, None, table[:, :], bass.IndirectOffsetOnAxis(ap=nodes, axis=0)
                                             ).then_inc(landed, 16)

            pool.wait_ge(s_index, 1)
            pool.wait_ge(s_hd, 16)
            for side, nodes in ((0, i_src), (1, i_dst)):
                for e in range(T_HH):
                    gather(hh_rows[:, 2 * side + e], h_dram, nodes[:, T_NODE + e:T_NODE + e + 1], s_hh_rows)

            def wait(what, value):
                pool.wait_ge(what, value)
                pool.sem_inc(s_turn, 1)

            def half_rows(table):
                return table.rearrange("n (h d) -> (n h) d", h=NHALF)

            def left_tile(t, row, s, first=False):
                if not first:
                    wait(s_left, t + (1 - SLOTS))
                nc.gpsimd.tensor_copy(index_now[:, s, 0:2], row).then_inc(s_halfnow, 1)
                wait(s_halfnow, t + 1)
                for n in range(2):
                    gather(edge_p[:, s, n * HALF:(n + 1) * HALF], left_tab[n], index_now[:, s, n:n + 1],
                           s_half[s])

            def take(t, row, s):
                nc.gpsimd.tensor_copy(index_now[:, s], row).then_inc(s_now, 1)
                wait(s_now, t + 2)

            def gather_tile(kind, s, right=False):
                for n, to in enumerate((edge_p, edge_q)):
                    tab, to = node_tab[kind][n], to[:, s]
                    if right:
                        tab, to = half_rows(tab), to[:, HALF:D]
                    gather(to, tab, index_now[:, s, n:n + 1], s_gath[s])

            def scatter(kind, s):
                nc.gpsimd.indirect_dma_start(pair_tab[kind][:, :], bass.IndirectOffsetOnAxis(ap=index_now[:, s, 2:3], axis=0),
                                             index_now[:, s, 3:4].bitcast(f32), None).then_inc(s_scat, 16)

            pool.wait_ge(s_leftst[0], 16)
            pool.wait_ge(s_leftst[1], 16)
            for t in range(SLOTS):
                left_tile(t, left_index[:, t], t, first=True)
            with pool.Fori(1, SPLIT_TILES // SLOTS) as i:
                for s in range(SLOTS):
                    left_tile(SLOTS * i + s, left_index[:, bass.ds(SLOTS * i + s, 1)].rearrange("p o c -> p (o c)"), s)
            pool.wait_ge(s_tabs, 48)
            pool.wait_ge(s_pst, 32)
            pool.wait_ge(s_qst, 32)
            pool.wait_ge(s_tr, 2 * KT)
            def load_table(kind):
                name = ("ho", "oo", "hh")[kind]
                pool.dma_start(tab_sb[kind], pair_tab[name].rearrange("(b p n) o -> p b (n o)", p=P, n=N)
                               ).then_inc(s_tab[kind], 16)

            def next_tile(t, row, s, first=False, right=False):
                wait(s_logit, t + (1 - SLOTS))
                take(t, row, s)
                gather_tile("ho", s, right)
                if not first:
                    wait(s_scat, 16 * t - 16 * SLOTS)
                scatter("ho", s)

            for t in range(SLOTS):
                pool.wait_ge(s_left, SPLIT_TILES - SLOTS + t + 1)
                take(t, index[:, t], t)
                gather_tile("ho", t)
            for t in range(SLOTS, 2 * SLOTS):
                next_tile(t, index[:, t], t % SLOTS, first=t == SLOTS)
            for first, last in ((2 * SLOTS, SPLIT_0), (SPLIT_0, SPLIT_0 + SPLIT_TILES), (SPLIT_0 + SPLIT_TILES, T_HO)):
                with pool.Fori(first // SLOTS, last // SLOTS) as i:
                    for s in range(SLOTS):
                        next_tile(SLOTS * i + s, index[:, bass.ds(SLOTS * i + s, 1)].rearrange("p o c -> p (o c)"), s,
                                  right=first == SPLIT_0)
            pool.wait_ge(s_hhlog, 1)
            for e in range(T_HH):
                if e:
                    pool.wait_ge(s_hhscat, 16 * e)
                nc.gpsimd.indirect_dma_start(pair_tab["hh"][:, :],
                                             bass.IndirectOffsetOnAxis(ap=pair_hh[:, e:e + 1], axis=0),
                                             logit_hh[:, e:e + 1], None).then_inc(s_hhscat, 16)
            for t in range(T_HO, T_NODE + SLOTS):
                s = t % SLOTS
                pool.wait_ge(s_logit, t - SLOTS + 1)
                take(t, index[:, t], s)
                if t == T_HO:
                    pool.wait_ge(s_pst, 64)
                    pool.wait_ge(s_qst, 64)
                if t < T_NODE:
                    gather_tile("oo", s)
                pool.wait_ge(s_scat, 16 * (t - SLOTS))
                scatter("ho" if t - SLOTS < T_HO else "oo", s)
                if t == T_HO + 1:
                    pool.wait_ge(s_hhscat, 16 * T_HH)
                    load_table(2)
                if t == T_HO + SLOTS:
                    pool.wait_ge(s_scat, 16 * T_HO)
                    load_table(0)
            pool.wait_ge(s_scat, 16 * T_NODE)
            load_table(1)
            pool.wait_ge(s_weighed, 1)
            for b in ORDER:
                nc.gpsimd.tensor_tensor(tab_sb[0][:, b], tab_sb[0][:, b], tab_sb[2][:, b], ALU.add).then_inc(s_esums, 1)


def kernel(x, src, dst, L0_gnn_W_hh, L0_gnn_b_hh, L0_gnn_W_oo, L0_gnn_b_oo, L0_gnn_W_ho, L0_gnn_b_ho,
           L0_gnn_W_a, L0_gnn_b_a, L0_gnn_W_hn, L0_gnn_b_hn, L0_gnn_W_on, L0_gnn_b_on):
    import numpy as np
    import concourse.bacc as bacc
    from concourse.bass_utils import run_bass_kernel_spmd

    def chunks(w, first, n, half):
        w = np.asarray(w).reshape(2 * KT, P, NHALF, HALF)[first:first + n * KC, :, half]
        return w.reshape(n, KC, P, HALF).transpose(0, 2, 1, 3)

    order = [chunks(w, 0, 4, half) for w in (L0_gnn_W_ho, L0_gnn_W_oo, L0_gnn_W_hh) for half in range(NHALF)]
    order += [chunks(w, k, 1, half) for half in range(NHALF) for k in (0, KC) for w in (L0_gnn_W_hn, L0_gnn_W_on)]
    order += [chunks(w, KT, 2, half) for w in (L0_gnn_W_on, L0_gnn_W_hn) for half in range(NHALF)]
    arrays = {
        "x": np.ascontiguousarray(x), "src": np.ascontiguousarray(src), "dst": np.ascontiguousarray(dst),
        "w_chunks": np.ascontiguousarray(np.concatenate(order)),
        "biases": np.stack([np.asarray(b) for b in (L0_gnn_b_ho, L0_gnn_b_oo, L0_gnn_b_hh, L0_gnn_b_hn, L0_gnn_b_on)]),
        "w_a": np.ascontiguousarray(np.asarray(L0_gnn_W_a).reshape(1, D)),
        "b_a": np.ascontiguousarray(np.asarray(L0_gnn_b_a).reshape(1, 1)),
    }
    nc = bacc.Bacc("TRN2", target_bir_lowering=False, num_devices=1)
    args = [nc.dram_tensor(name, a.shape, mybir.dt.from_np(a.dtype), kind="ExternalInput").ap()
            for name, a in arrays.items()]
    out = nc.dram_tensor("out", (N, D), mybir.dt.float32, kind="ExternalOutput").ap()
    build(nc, *args, out)
    return run_bass_kernel_spmd(nc, [arrays], core_ids=[0]).results[0]["out"]
```
